# Optimizing a Trainium2 kernel written in Bass

```python
import numpy as np
import jax
import jax.numpy as jnp

def _softmax(x, axis=-1):
    return jax.nn.softmax(x, axis=axis)

def _gelu(x):
    return jax.nn.gelu(x, approximate=True)

def _silu(x):
    return jax.nn.silu(x)

def _sigmoid(x):
    return jax.nn.sigmoid(x)

def _layernorm(x, axis=-1, eps=1e-05):
    m = jnp.mean(x, axis=axis, keepdims=True)
    v = jnp.var(x, axis=axis, keepdims=True)
    return (x - m) / jnp.sqrt(v + eps)

def _scatter_add(tgt, idx, src, axis=0):
    return tgt.at[idx].add(src)

def _segment_sum(src, seg, n):
    return jax.ops.segment_sum(src, seg, n)
kernel_name = 'mk_gnn_ffn_d2_gnn_r8_ecdbe1'

def setup_inputs(seed: int=0):
    np.random.seed(seed)
    _w = jnp.asarray

    def _rec_inputs():
        import jax
        import jax.numpy as jnp
        _gk = jax.random.key(seed)
        x = -0.0001126 + 1 * jax.random.normal(jax.random.fold_in(_gk, 1), (3750, 256), jnp.float32)
        src = jax.random.randint(jax.random.fold_in(_gk, 2), (60000,), 0, 3750, jnp.int32)
        dst = jax.random.randint(jax.random.fold_in(_gk, 3), (60000,), 0, 3750, jnp.int32)
        _o = jnp.argsort(dst, stable=True)
        src = src[_o]
        dst = dst[_o]
        edge_type_8 = jax.random.randint(jax.random.fold_in(_gk, 13), (60000,), 0, 8, jnp.int32)
        return (x, src, dst, edge_type_8)
    x, src, dst, edge_type_8 = _rec_inputs()

    def _L0_gnn_setup():
        import jax, jax.numpy as jnp
        import numpy as np
        N_NODES = 3750
        N_EDGES = 60000
        IN_FEAT = 256
        OUT_FEAT = 256
        N_RELS = 8
        N_HEADS = 4
        HEAD_DIM = OUT_FEAT // N_HEADS
        LEAKY_SLOPE = 0.2
        key = jax.random.key(seed)
        ks = jax.random.split(key, 8)
        inputs = jax.random.normal(ks[0], (N_NODES, IN_FEAT), dtype=jnp.float32)
        conv_weights = jax.random.normal(ks[1], (N_RELS, N_HEADS, IN_FEAT, HEAD_DIM), dtype=jnp.float32) * (1.0 / np.sqrt(IN_FEAT))
        attn_l = jax.random.normal(ks[2], (N_RELS, N_HEADS, HEAD_DIM), dtype=jnp.float32) * 0.1
        attn_r = jax.random.normal(ks[3], (N_RELS, N_HEADS, HEAD_DIM), dtype=jnp.float32) * 0.1
        h_bias = jax.random.normal(ks[4], (OUT_FEAT,), dtype=jnp.float32) * 0.02
        edge_src = jax.random.randint(ks[5], (N_EDGES,), 0, N_NODES, dtype=jnp.int32)
        edge_dst = jax.random.randint(ks[6], (N_EDGES,), 0, N_NODES, dtype=jnp.int32)
        edge_type = jax.random.randint(ks[7], (N_EDGES,), 0, N_RELS, dtype=jnp.int32)
        return {'inputs': inputs, 'conv_weights': conv_weights, 'attn_l': attn_l, 'attn_r': attn_r, 'h_bias': h_bias, 'edge_src': edge_src, 'edge_dst': edge_dst, 'edge_type': edge_type}
    _L0_gnn_all = _L0_gnn_setup()
    _L0_gnn_in = {k: v for k, v in _L0_gnn_all.items() if k in ('conv_weights', 'attn_l', 'attn_r', 'h_bias')}
    del _L0_gnn_all

    def _L0_ffn_setup():
        import jax, jax.numpy as jnp
        import numpy as np
        E = 8
        K = 2
        D = 256
        H = 512
        DOUT = 256
        EPS = 1e-05
        key = jax.random.key(seed)
        ks = jax.random.split(key, 9)
        s = 0.02
        return {'x': jax.random.normal(ks[0], (4, 1024, D), jnp.float32), 'gamma': 1.0 + 0.05 * jax.random.normal(ks[1], (D,), jnp.float32), 'beta': 0.05 * jax.random.normal(ks[2], (D,), jnp.float32), 'Wr': 0.01 * jax.random.normal(ks[3], (D, E), jnp.float32), 'br': jnp.zeros((E,), jnp.float32), 'W1': s * jax.random.normal(ks[4], (E, D, H), jnp.float32), 'b1': s * jax.random.normal(ks[5], (E, H), jnp.float32), 'W2': s * jax.random.normal(ks[6], (E, H, DOUT), jnp.float32), 'b2': s * jax.random.normal(ks[7], (E, DOUT), jnp.float32)}
    _L0_ffn_all = _L0_ffn_setup()
    _L0_ffn_in = {k: v for k, v in _L0_ffn_all.items() if k in ('gamma', 'beta', 'Wr', 'br', 'W1', 'b1', 'W2', 'b2')}
    del _L0_ffn_all

    def _L1_gnn_setup():
        import jax, jax.numpy as jnp
        import numpy as np
        N_ENT = 6250
        N_EDGE = 62500
        D = 256
        H1, C1 = (8, 64)
        NEG_SLOPE = 0.2
        LN_EPS = 1e-05

        def _gat_conv(x, edge_index, W, att_src, att_dst, bias, heads, out_ch, concat):
            n = x.shape[0]
            loops = jnp.arange(n)
            src = jnp.concatenate([edge_index[0], loops])
            dst = jnp.concatenate([edge_index[1], loops])
            h = (x @ W).reshape(n, heads, out_ch)
            a_src = jnp.sum(h * att_src[None], axis=-1)
            a_dst = jnp.sum(h * att_dst[None], axis=-1)
            e = jax.nn.leaky_relu(a_src[src] + a_dst[dst], NEG_SLOPE)
            m = jax.lax.stop_gradient(jax.ops.segment_max(e, dst, num_segments=n))
            p = jnp.exp(e - m[dst])
            denom = jax.ops.segment_sum(p, dst, num_segments=n)
            alpha = p / denom[dst]
            out = jax.ops.segment_sum(h[src] * alpha[..., None], dst, num_segments=n)
            out = out.reshape(n, heads * out_ch) if concat else out.mean(axis=1)
            return out + bias
        key = jax.random.key(seed)
        ks = jax.random.split(key, 12)
        s = 0.05
        return {'edge_index': jax.random.randint(ks[0], (2, N_EDGE), 0, N_ENT), 'x': jax.random.normal(ks[1], (N_ENT, D), dtype=jnp.float32), 'ln_w': jnp.ones((D,), jnp.float32), 'ln_b': jnp.zeros((D,), jnp.float32), 'W1': jax.random.normal(ks[2], (D, H1 * C1), dtype=jnp.float32) * s, 'att_src1': jax.random.normal(ks[3], (H1, C1), dtype=jnp.float32) * s, 'att_dst1': jax.random.normal(ks[4], (H1, C1), dtype=jnp.float32) * s, 'b1': jnp.zeros((H1 * C1,), jnp.float32), 'W2': jax.random.normal(ks[5], (H1 * C1, D), dtype=jnp.float32) * s, 'att_src2': jax.random.normal(ks[6], (1, D), dtype=jnp.float32) * s, 'att_dst2': jax.random.normal(ks[7], (1, D), dtype=jnp.float32) * s, 'b2': jnp.zeros((D,), jnp.float32)}
    _L1_gnn_all = _L1_gnn_setup()
    _L1_gnn_in = {k: v for k, v in _L1_gnn_all.items() if k in ('ln_w', 'ln_b', 'W1', 'att_src1', 'att_dst1', 'b1', 'W2', 'att_src2', 'att_dst2', 'b2')}
    del _L1_gnn_all

    def _L1_ffn_setup():
        import jax, jax.numpy as jnp
        import numpy as np
        BN_EPS = 0.001

        def _bn(h, g, b, m, v):
            return g * (h - m) * jax.lax.rsqrt(v + BN_EPS) + b
        key = jax.random.key(seed)
        ks = jax.random.split(key, 8)
        B, F, Df = (256, 64, 256)
        E, H, D = (8, 256, 256)
        s1 = 1.0 / np.sqrt(Df)
        s2 = 1.0 / np.sqrt(H)
        return {'x': jax.random.normal(ks[0], (B, F, Df), jnp.float32), 'Wr': jax.random.normal(ks[1], (Df, E), jnp.float32) * s1, 'br': jnp.zeros((E,), jnp.float32), 'W1': jax.random.normal(ks[2], (E, Df, H), jnp.float32) * s1, 'b1': jnp.zeros((E, H), jnp.float32), 'g1': jnp.ones((E, H), jnp.float32), 'be1': jnp.zeros((E, H), jnp.float32), 'm1': jnp.zeros((E, H), jnp.float32), 'v1': jnp.ones((E, H), jnp.float32), 'W2': jax.random.normal(ks[3], (E, H, H), jnp.float32) * s2, 'b2': jnp.zeros((E, H), jnp.float32), 'g2': jnp.ones((E, H), jnp.float32), 'be2': jnp.zeros((E, H), jnp.float32), 'm2': jnp.zeros((E, H), jnp.float32), 'v2': jnp.ones((E, H), jnp.float32), 'Wo': jax.random.normal(ks[4], (E, H, D), jnp.float32) * s2, 'bo': jnp.zeros((E, D), jnp.float32)}
    _L1_ffn_all = _L1_ffn_setup()
    _L1_ffn_in = {k: v for k, v in _L1_ffn_all.items() if k in ('Wr', 'br', 'W1', 'b1', 'g1', 'be1', 'm1', 'v1', 'W2', 'b2', 'g2', 'be2', 'm2', 'v2', 'Wo', 'bo')}
    del _L1_ffn_all
    return {'x': x, 'src': src, 'dst': dst, 'edge_type_8': edge_type_8, 'L0_gnn_conv_weights': _L0_gnn_in['conv_weights'], 'L0_gnn_attn_l': _L0_gnn_in['attn_l'], 'L0_gnn_attn_r': _L0_gnn_in['attn_r'], 'L0_gnn_h_bias': _L0_gnn_in['h_bias'], 'L0_ffn_gamma': _L0_ffn_in['gamma'], 'L0_ffn_beta': _L0_ffn_in['beta'], 'L0_ffn_Wr': _L0_ffn_in['Wr'], 'L0_ffn_br': _L0_ffn_in['br'], 'L0_ffn_W1': _L0_ffn_in['W1'], 'L0_ffn_b1': _L0_ffn_in['b1'], 'L0_ffn_W2': _L0_ffn_in['W2'], 'L0_ffn_b2': _L0_ffn_in['b2'], 'L1_gnn_ln_w': _L1_gnn_in['ln_w'], 'L1_gnn_ln_b': _L1_gnn_in['ln_b'], 'L1_gnn_W1': _L1_gnn_in['W1'], 'L1_gnn_att_src1': _L1_gnn_in['att_src1'], 'L1_gnn_att_dst1': _L1_gnn_in['att_dst1'], 'L1_gnn_b1': _L1_gnn_in['b1'], 'L1_gnn_W2': _L1_gnn_in['W2'], 'L1_gnn_att_src2': _L1_gnn_in['att_src2'], 'L1_gnn_att_dst2': _L1_gnn_in['att_dst2'], 'L1_gnn_b2': _L1_gnn_in['b2'], 'L1_ffn_Wr': _L1_ffn_in['Wr'], 'L1_ffn_br': _L1_ffn_in['br'], 'L1_ffn_W1': _L1_ffn_in['W1'], 'L1_ffn_b1': _L1_ffn_in['b1'], 'L1_ffn_g1': _L1_ffn_in['g1'], 'L1_ffn_be1': _L1_ffn_in['be1'], 'L1_ffn_m1': _L1_ffn_in['m1'], 'L1_ffn_v1': _L1_ffn_in['v1'], 'L1_ffn_W2': _L1_ffn_in['W2'], 'L1_ffn_b2': _L1_ffn_in['b2'], 'L1_ffn_g2': _L1_ffn_in['g2'], 'L1_ffn_be2': _L1_ffn_in['be2'], 'L1_ffn_m2': _L1_ffn_in['m2'], 'L1_ffn_v2': _L1_ffn_in['v2'], 'L1_ffn_Wo': _L1_ffn_in['Wo'], 'L1_ffn_bo': _L1_ffn_in['bo']}

def reference(x, src, dst, edge_type_8, L0_gnn_conv_weights, L0_gnn_attn_l, L0_gnn_attn_r, L0_gnn_h_bias, L0_ffn_gamma, L0_ffn_beta, L0_ffn_Wr, L0_ffn_br, L0_ffn_W1, L0_ffn_b1, L0_ffn_W2, L0_ffn_b2, L1_gnn_ln_w, L1_gnn_ln_b, L1_gnn_W1, L1_gnn_att_src1, L1_gnn_att_dst1, L1_gnn_b1, L1_gnn_W2, L1_gnn_att_src2, L1_gnn_att_dst2, L1_gnn_b2, L1_ffn_Wr, L1_ffn_br, L1_ffn_W1, L1_ffn_b1, L1_ffn_g1, L1_ffn_be1, L1_ffn_m1, L1_ffn_v1, L1_ffn_W2, L1_ffn_b2, L1_ffn_g2, L1_ffn_be2, L1_ffn_m2, L1_ffn_v2, L1_ffn_Wo, L1_ffn_bo):
    import jax
    import jax.numpy as jnp

    def _L0_gnn_ref(inputs, conv_weights, attn_l, attn_r, h_bias, edge_src, edge_dst, edge_type):
        import jax, jax.numpy as jnp
        import numpy as np
        N_NODES = 3750
        N_EDGES = 60000
        IN_FEAT = 256
        OUT_FEAT = 256
        N_RELS = 8
        N_HEADS = 4
        HEAD_DIM = OUT_FEAT // N_HEADS
        LEAKY_SLOPE = 0.2
        feat_all = jnp.einsum('ni,rhid->rnhd', inputs, conv_weights)
        feat_src_e = feat_all[edge_type, edge_src]
        feat_dst_e = feat_all[edge_type, edge_dst]
        el = jnp.sum(feat_src_e * attn_l[edge_type], axis=-1)
        er = jnp.sum(feat_dst_e * attn_r[edge_type], axis=-1)
        e = jax.nn.leaky_relu(el + er, negative_slope=LEAKY_SLOPE)
        m = jax.ops.segment_max(e, edge_dst, num_segments=N_NODES)
        ex = jnp.exp(e - m[edge_dst])
        denom = jax.ops.segment_sum(ex, edge_dst, num_segments=N_NODES)
        alpha = ex / denom[edge_dst]
        h = jax.ops.segment_sum(alpha[..., None] * feat_src_e, edge_dst, num_segments=N_NODES)
        h = h.reshape(N_NODES, OUT_FEAT) + h_bias
        return h

    def _L0_ffn_ref(x, gamma, beta, Wr, br, W1, b1, W2, b2):
        import jax, jax.numpy as jnp
        import numpy as np
        E = 8
        K = 2
        D = 256
        H = 512
        DOUT = 256
        EPS = 1e-05
        mu = jnp.mean(x, axis=-1, keepdims=True)
        var = jnp.mean(jnp.square(x - mu), axis=-1, keepdims=True)
        xn = (x - mu) * jax.lax.rsqrt(var + EPS) * gamma + beta
        logits = jnp.einsum('bsd,de->bse', xn, Wr) + br
        top_vals, top_idx = jax.lax.top_k(logits, K)
        w = jax.nn.softmax(top_vals, axis=-1)
        w_full = jnp.einsum('bsk,bske->bse', w, jax.nn.one_hot(top_idx, E, dtype=w.dtype))
        y = jnp.zeros(x.shape[:-1] + (DOUT,), x.dtype)
        for e in range(E):
            h = jax.nn.gelu(jnp.einsum('bsd,dh->bsh', xn, W1[e]) + b1[e], approximate=False)
            y_e = jnp.einsum('bsh,hd->bsd', h, W2[e]) + b2[e]
            y = y + y_e * w_full[..., e, None]
        return y

    def _L1_gnn_ref(edge_index, x, ln_w, ln_b, W1, att_src1, att_dst1, b1, W2, att_src2, att_dst2, b2):
        import jax, jax.numpy as jnp
        import numpy as np
        N_ENT = 6250
        N_EDGE = 62500
        D = 256
        H1, C1 = (8, 64)
        NEG_SLOPE = 0.2
        LN_EPS = 1e-05

        def _gat_conv(x, edge_index, W, att_src, att_dst, bias, heads, out_ch, concat):
            n = x.shape[0]
            loops = jnp.arange(n)
            src = jnp.concatenate([edge_index[0], loops])
            dst = jnp.concatenate([edge_index[1], loops])
            h = (x @ W).reshape(n, heads, out_ch)
            a_src = jnp.sum(h * att_src[None], axis=-1)
            a_dst = jnp.sum(h * att_dst[None], axis=-1)
            e = jax.nn.leaky_relu(a_src[src] + a_dst[dst], NEG_SLOPE)
            m = jax.lax.stop_gradient(jax.ops.segment_max(e, dst, num_segments=n))
            p = jnp.exp(e - m[dst])
            denom = jax.ops.segment_sum(p, dst, num_segments=n)
            alpha = p / denom[dst]
            out = jax.ops.segment_sum(h[src] * alpha[..., None], dst, num_segments=n)
            out = out.reshape(n, heads * out_ch) if concat else out.mean(axis=1)
            return out + bias
        mu = jnp.mean(x, axis=-1, keepdims=True)
        var = jnp.var(x, axis=-1, keepdims=True)
        h = (x - mu) / jnp.sqrt(var + LN_EPS) * ln_w + ln_b
        h = jax.nn.elu(_gat_conv(h, edge_index, W1, att_src1, att_dst1, b1, H1, C1, True))
        return _gat_conv(h, edge_index, W2, att_src2, att_dst2, b2, 1, D, False)

    def _L1_ffn_ref(x, Wr, br, W1, b1, g1, be1, m1, v1, W2, b2, g2, be2, m2, v2, Wo, bo):
        import jax, jax.numpy as jnp
        import numpy as np
        BN_EPS = 0.001

        def _bn(h, g, b, m, v):
            return g * (h - m) * jax.lax.rsqrt(v + BN_EPS) + b
        feat = jnp.mean(x, axis=0)
        w = jax.nn.softmax(feat @ Wr + br, axis=-1)
        h = jnp.einsum('bfd,edh->bfeh', x, W1) + b1
        h = jax.nn.relu(_bn(h, g1, be1, m1, v1))
        h = jnp.einsum('bfeh,ehk->bfek', h, W2) + b2
        h = jax.nn.relu(_bn(h, g2, be2, m2, v2))
        y = jnp.einsum('bfeh,ehd->bfed', h, Wo) + bo
        return jnp.einsum('bfed,fe->bfd', y, w)
    edge_index = jnp.stack([src, dst])
    x = x + _L0_gnn_ref(_layernorm(x, axis=-1), L0_gnn_conv_weights, L0_gnn_attn_l, L0_gnn_attn_r, L0_gnn_h_bias, src, dst, edge_type_8)
    x = x + _L0_ffn_ref(_layernorm(x, axis=-1)[None], L0_ffn_gamma, L0_ffn_beta, L0_ffn_Wr, L0_ffn_br, L0_ffn_W1, L0_ffn_b1, L0_ffn_W2, L0_ffn_b2)[0]
    x = x + _L1_gnn_ref(edge_index, _layernorm(x, axis=-1), L1_gnn_ln_w, L1_gnn_ln_b, L1_gnn_W1, L1_gnn_att_src1, L1_gnn_att_dst1, L1_gnn_b1, L1_gnn_W2, L1_gnn_att_src2, L1_gnn_att_dst2, L1_gnn_b2)
    x = x + _L1_ffn_ref(_layernorm(x, axis=-1)[None], L1_ffn_Wr, L1_ffn_br, L1_ffn_W1, L1_ffn_b1, L1_ffn_g1, L1_ffn_be1, L1_ffn_m1, L1_ffn_v1, L1_ffn_W2, L1_ffn_b2, L1_ffn_g2, L1_ffn_be2, L1_ffn_m2, L1_ffn_v2, L1_ffn_Wo, L1_ffn_bo)[0]
    return x

_drawn_inputs = setup_inputs


def setup_inputs(seed=0):
    import zlib

    import numpy as np

    out = dict(_drawn_inputs(seed))
    spreads = {'L0_ffn_br': (0.0, 0.1),
     'L1_gnn_ln_w': (1.0, 0.6),
     'L1_gnn_ln_b': (0.0, 0.1),
     'L1_gnn_b1': (0.0, 0.1),
     'L1_gnn_b2': (0.0, 0.1),
     'L1_ffn_br': (0.0, 0.538),
     'L1_ffn_b1': (0.0, 0.322),
     'L1_ffn_g1': (1.0, 0.2),
     'L1_ffn_be1': (0.0, 0.357),
     'L1_ffn_m1': (0.0, 0.335),
     'L1_ffn_v1': (1.0, 0.6),
     'L1_ffn_b2': (0.0, 0.1),
     'L1_ffn_g2': (1.0, 0.2),
     'L1_ffn_be2': (0.0, 0.281),
     'L1_ffn_m2': (0.0, 0.1),
     'L1_ffn_v2': (1.0, 0.6),
     'L1_ffn_bo': (0.0, 0.1)}
    factors = {'L0_ffn_gamma': 6.34,
     'L0_ffn_beta': 5.093,
     'L0_ffn_b1': 8.0,
     'L0_ffn_b2': 3.858,
     'L1_gnn_att_dst1': 8.0,
     'L1_gnn_att_src2': 6.311,
     'L1_gnn_att_dst2': 8.0}
    for name, (base, spread) in spreads.items():
        noise = np.random.default_rng([zlib.crc32(name.encode()), seed]).standard_normal(out[name].shape)
        drawn = base * np.exp(spread * noise) if base else spread * noise
        out[name] = jnp.asarray(drawn.astype(out[name].dtype))
    for name, factor in factors.items():
        out[name] = (out[name] * factor).astype(out[name].dtype)
    return out
```

```python
from contextlib import ExitStack

import concourse.bass as bass
from concourse import mybir

F32 = mybir.dt.float32
I32 = mybir.dt.int32
U32 = mybir.dt.uint32
ALU = mybir.AluOpType
ACT = mybir.ActivationFunctionType
AX_X = mybir.AxisListType.X
ds = bass.ds

P = 128
N, D, E, R = 3750, 256, 60000, 8
T = -(-N // P)
NP = T * P
LAST = N - (T - 1) * P
COLS = 512
ROWS = -(-E // COLS)
TAIL = E - (ROWS - 1) * COLS
KB = COLS // P
C = ROWS * KB
G = 2
CU = -(-E // (P * G)) * G
CG = CU // G
STEPS = CG + T - 1
FAR = 1.0e30
SLOPE = 0.2
EPS = 1e-5
STOP = 99
BATCH = 5
U = 4
assert CU % (2 * BATCH) == 0 and STEPS % U == 0 and T % 2 == 0


class Steps:

    def __init__(self, engine, sem, base=0):
        self.engine, self.sem, self.base, self.n = engine, sem, base, 0

    def __call__(self, ins):
        ins.then_inc(self.sem, 1)
        self.n += 1
        self.engine.wait_ge(self.sem, self.base + self.n)
        return ins


class Phase:

    def __init__(self, nc, name):
        self.nc, self.name, self.ctx = nc, name, ExitStack()
        self.inner, self.sems = ExitStack(), []

    def __enter__(self):
        return self

    def __exit__(self, *a):
        self.inner.__exit__(*a)
        if a[0] is None:
            for s in self.sems:
                self.nc.gpsimd.sem_clear(s)
            self.nc.all_engine_barrier()
        return self.ctx.__exit__(*a)

    def sb(self, name, shape, dt=F32):
        return self.ctx.enter_context(self.nc.sbuf_tensor(f"{self.name}_{name}", shape, dt))

    def ps(self, name, shape, dt=F32):
        return self.ctx.enter_context(self.nc.psum_tensor(f"{self.name}_{name}", shape, dt))

    def sem(self, name):
        self.sems.append(self.ctx.enter_context(self.nc.semaphore(f"{self.name}_{name}")))
        return self.sems[-1]

    def gathers(self, g, n):
        return [g.ctx.enter_context(self.nc.semaphore(f"{self.name}_landed{u}")) for u in range(n)]

    def block(self):
        return self.inner.enter_context(self.nc.Block())


def row_of(vector, parts=P):
    return vector.rearrange("(a d) -> a d", a=1).to_broadcast([parts, vector.shape[0]])


def normed(nc, g, link, out, t):
    link(nc.vector.tensor_scalar(out, g.x[:, ds(t, 1), :].rearrange("p a f -> p (a f)"),
                                 g.mean[:, ds(t, 1)], g.rstd[:, ds(t, 1)], ALU.subtract, ALU.mult))


def node_stats(nc, g, name, twice, loads=(), alloc=None, update=None):
    with Phase(nc, name + "_stats") as ph:
        step, loaded, var_ready, rooted = (ph.sem(s) for s in ("step", "loaded", "var_ready", "rooted"))
        raw = ph.sb("raw", [P, T, 6])
        stat = ph.sb("stat", [P, T, 2])
        root, again = ph.sb("root", [P, T]), ph.sb("again", [P, T])
        pairs = alloc(ph) if alloc else []
        block = ph.block()

        @block.sync
        def _(sp):
            for out, src in pairs:
                sp.dma_start(out, src).then_inc(loaded, 16)

        @block.vector
        def _(dve):
            link = Steps(dve, step)
            if update:
                dve.wait_ge(loaded, 16 * len(pairs))
                update(dve, link, [out for out, _ in pairs])
            base = link.n
            with dve.Fori(0, T) as t:
                nc.vector.bn_stats(raw[:, ds(t, 1), :].rearrange("p a s -> p (a s)"),
                                   g.x[:, ds(t, 1), :].rearrange("p a f -> p (a f)")).then_inc(step, 1)
            link = Steps(dve, step, base + T)
            dve.wait_ge(step, base + T)
            half, square = stat[:, :, 0], stat[:, :, 1]
            link(nc.vector.tensor_tensor(half, raw[:, :, 1], raw[:, :, 4], ALU.add))
            link(nc.vector.tensor_scalar(g.mean[:, :], half, 0.5, None, ALU.mult))
            link(nc.vector.tensor_tensor(half, raw[:, :, 1], raw[:, :, 4], ALU.subtract))
            link(nc.vector.tensor_scalar(half, half, 0.5, None, ALU.mult))
            link(nc.vector.tensor_tensor(half, half, half, ALU.mult))
            link(nc.vector.tensor_tensor(square, raw[:, :, 2], raw[:, :, 5], ALU.add))
            link(nc.vector.scalar_tensor_tensor(out=square, in0=square, scalar=1.0 / D, in1=half, op0=ALU.mult, op1=ALU.add))
            link(nc.vector.tensor_scalar(root[:, :], stat[:, :, 1], EPS, None, ALU.add))
            dve.sem_inc(var_ready, 1)
            dve.wait_ge(rooted, 1)
            link(nc.vector.reciprocal(g.rstd[:, :], root[:, :]))
            if twice:
                link(nc.vector.tensor_tensor(again[:, :], g.rstd[:, :], g.rstd[:, :], ALU.mult))
                link(nc.vector.tensor_tensor(again[:, :], again[:, :], stat[:, :, 1], ALU.mult))
                link(nc.vector.tensor_scalar(root[:, :], again[:, :], EPS, None, ALU.add))
                dve.sem_inc(var_ready, 1)
                dve.wait_ge(rooted, 2)
                link(nc.vector.reciprocal(again[:, :], root[:, :]))
                link(nc.vector.tensor_tensor(g.rstd[:, :], g.rstd[:, :], again[:, :], ALU.mult))

        @block.scalar
        def _(act):
            for r in range(2 if twice else 1):
                act.wait_ge(var_ready, r + 1)
                nc.scalar.activation(root[:, :], root[:, :], ACT.Sqrt).then_inc(rooted, 1)


def setup(nc, g, x, src, dst, etype):
    with Phase(nc, "setup") as ph:
        sb, sem = ph.sb, ph.sem
        dstx = sb("dstx", [ROWS, COLS + 2], I32)
        srca = sb("srca", [ROWS, COLS], I32)
        typa = sb("typa", [ROWS, COLS], I32)
        fa = sb("fa", [ROWS, 4, COLS])
        dstf = sb("dstf", [ROWS, COLS + 2])
        pcol = sb("pcol", [P, 1])
        rowc = sb("rowc", [ROWS, 2, 8])
        tli = sb("tli", [ROWS, KB // G], I32)
        key = sb("key", [ROWS, KB // G])
        cmp = sb("cmp", [ROWS, KB // G, STEPS])
        ones = sb("ones", [P, 1])
        tps = [ph.ps(f"tps{a}", [P, KB, P]) for a in range(4)]
        rps = ph.ps("rps", [8, 2, P])
        cps = ph.ps("cps", [1, 512])
        filled, loaded, xloaded = sem("filled"), sem("loaded"), sem("xloaded")
        made, step, fready, turned = sem("made"), sem("step"), sem("fready"), sem("turned")
        identr, cmpr, counted = sem("identr"), sem("cmpr"), sem("counted")
        block = ph.block()

        @block.sync
        def _(sp):
            sp.dma_start(g.x[:, 0:T - 1, :], x[0:(T - 1) * P, :].rearrange("(t p) f -> p t f", p=P)).then_inc(xloaded, 16)
            sp.wait_ge(filled, 4)
            sp.dma_start(g.x[0:LAST, T - 1, :], x[(T - 1) * P:N, :]).then_inc(xloaded, 16)
            full = (ROWS - 1) * COLS
            for tile, vec in ((dstx[:, 1:COLS + 1], dst), (srca[:, :], src), (typa[:, :], etype)):
                sp.dma_start(tile[0:ROWS - 1, :], vec[0:full].rearrange("(r c) -> r c", c=COLS)).then_inc(loaded, 16)
                sp.dma_start(tile[ROWS - 1:ROWS, 0:TAIL], vec[full:E].rearrange("(r c) -> r c", r=1)).then_inc(loaded, 16)
            with nc.allow_non_contiguous_dma(reason="one edge of each row"):
                sp.dma_start(dstx[1:ROWS, 0:1], dst[0:full].rearrange("(r c) -> r c", c=COLS)[:, COLS - 1:COLS]).then_inc(loaded, 16)
                sp.dma_start(dstx[0:ROWS - 2, COLS + 1:COLS + 2],
                             dst[0:full].rearrange("(r c) -> r c", c=COLS)[1:ROWS - 1, 0:1]).then_inc(loaded, 16)
                sp.dma_start(dstx[ROWS - 2:ROWS - 1, COLS + 1:COLS + 2],
                             dst[full:full + 1].rearrange("(r c) -> r c", c=1)).then_inc(loaded, 16)
            sp.wait_ge(loaded, 16 * 9)
            sp.wait_ge(xloaded, 32)

        @block.gpsimd
        def _(pool):
            nc.gpsimd.memset(g.x[:, T - 1, :], 0.0).then_inc(filled, 1)
            nc.gpsimd.memset(dstx[:, :], NP - 1).then_inc(filled, 1)
            nc.gpsimd.memset(srca[:, :], 0).then_inc(filled, 1)
            nc.gpsimd.memset(typa[:, :], 0).then_inc(filled, 1)
            nc.gpsimd.iota(pcol[:, :], [[0, 1]], base=0, channel_multiplier=1,
                           allow_small_or_imprecise_dtypes=True).then_inc(made, 1)
            nc.gpsimd.iota(g.nodes[:, :], [[1, NP]], base=0, channel_multiplier=0,
                           allow_small_or_imprecise_dtypes=True).then_inc(made, 1)
            nc.gpsimd.iota(key[:, :], [[1, KB // G]], base=0, channel_multiplier=KB // G,
                           allow_small_or_imprecise_dtypes=True).then_inc(made, 1)

        @block.vector
        def _(dve):
            link = Steps(dve, step)
            dve.wait_ge(made, 3)
            nc.vector.tensor_scalar(g.ident[:, :], g.nodes[:, 0:P], pcol[:, 0:1], None, ALU.is_equal).then_inc(identr, 1)
            link(nc.vector.memset(ones[:, :], 1.0))
            dve.wait_ge(loaded, 16 * 9)
            link(nc.vector.tensor_copy(dstf[:, :], dstx[:, :]))
            nc.vector.tensor_copy(fa[:, 0, :], dstf[:, 1:COLS + 1]).then_inc(fready, 1)
            nc.vector.tensor_copy(fa[:, 1, :], srca[:, :]).then_inc(fready, 1)
            nc.vector.scalar_tensor_tensor(out=fa[:, 2, :], in0=srca[:, :], scalar=float(R), in1=typa[:, :],
                                           op0=ALU.mult, op1=ALU.add).then_inc(fready, 1)
            nc.vector.scalar_tensor_tensor(out=fa[:, 3, :], in0=dstx[:, 1:COLS + 1], scalar=float(R), in1=typa[:, :],
                                           op0=ALU.mult, op1=ALU.add).then_inc(fready, 1)
            link(nc.vector.tensor_tensor(g.same[:, :], dstf[:, 0:COLS + 1], dstf[:, 1:COLS + 2], ALU.is_equal))
            link(nc.vector.tensor_scalar(g.apart[:, :], g.same[:, :], 1.0, FAR, ALU.subtract, ALU.mult))
            nc.vector.tensor_tensor(rowc[:, 0, :], dstf[:, 0:1].to_broadcast([ROWS, 8]),
                                    dstf[:, COLS:COLS + 1].to_broadcast([ROWS, 8]), ALU.is_equal).then_inc(fready, 1)
            nc.vector.tensor_tensor(rowc[:, 1, :], dstf[:, 1:2].to_broadcast([ROWS, 8]),
                                    dstf[:, COLS + 1:COLS + 2].to_broadcast([ROWS, 8]), ALU.is_equal).then_inc(fready, 1)
            link(nc.vector.tensor_scalar(tli[:, :], dstx[:, 1:COLS + 1].rearrange("r (k c) -> r k c", c=G * P)[:, :, G * P - 1],
                                         7, None, ALU.arith_shift_right))
            link(nc.vector.tensor_tensor(key[:, :], key[:, :], tli[:, :], ALU.add))
            for k in range(KB // G):
                ins = nc.vector.tensor_scalar(cmp[:, k, :], g.nodes[0:ROWS, 0:STEPS], key[:, k:k + 1], None, ALU.is_gt)
            ins.then_inc(cmpr, 1)
            outs = ((g.dstb, g.dsti), (None, g.srci), (None, g.srct), (None, g.dstt))
            for a, (flt, integer) in enumerate(outs):
                dve.wait_ge(turned, a + 1)
                for out in (flt, integer):
                    if out is not None:
                        link(nc.vector.tensor_copy(out[:, :].rearrange("q (r k) -> q k r", k=KB), tps[a][:, :, 0:ROWS]))
            dve.wait_ge(turned, 5)
            link(nc.vector.tensor_copy(g.rowsame[:, :, :], rps[:, :, 0:ROWS]))
            link(nc.vector.tensor_scalar(g.rowapart[:, :, :], g.rowsame[:, :, :], 1.0, FAR, ALU.subtract, ALU.mult))
            dve.wait_ge(counted, 1)
            link(nc.vector.tensor_copy(g.walk[:, :, 0], cps[0:1, 0:STEPS]))
            link(nc.vector.tensor_tensor(g.walk[:, :, 1], g.nodes[0:1, 0:STEPS], cps[0:1, 0:STEPS], ALU.subtract))

        @block.tensor
        def _(pe):
            pe.wait_ge(identr, 1)
            for a in range(4):
                pe.wait_ge(fready, a + 1)
                for k in range(KB):
                    ins = nc.tensor.transpose(tps[a][:, k, 0:ROWS], fa[:, a, k * P:(k + 1) * P], g.ident[0:ROWS, 0:ROWS])
                ins.then_inc(turned, 1)
            pe.wait_ge(fready, 6)
            for a in range(2):
                ins = nc.tensor.transpose(rps[:, a, 0:ROWS], rowc[:, a, :], g.ident[0:ROWS, 0:ROWS])
            ins.then_inc(turned, 1)
            pe.wait_ge(cmpr, 1)
            for k in range(KB // G):
                ins = nc.tensor.matmul(cps[0:1, 0:STEPS], ones[0:ROWS, :], cmp[:, k, :], start=(k == 0), stop=(k == KB // G - 1))
            ins.then_inc(counted, 1)


def project(nc, g, name, kc, f, heads, wload, attload, prep, table, tabs, tabd, selfloop, extra):
    hw = f // heads
    na = 2 * heads
    with Phase(nc, name) as ph:
        sb, sem = ph.sb, ph.sem
        w = sb("w", [P, kc, f])
        att_b = sb("att", [P, 2, f])
        prod = sb("prod", [P, f])
        wa = sb("wa", [P, kc, na])
        rows = [sb(f"rows{u}", [P, kc * P]) for u in range(2)]
        turned = [sb(f"turned{u}", [P, kc, P]) for u in range(2)]
        stage = [sb(f"stage{u}", [P, f]) for u in range(2)]
        lstage = [sb(f"lstage{u}", [P, na + heads]) for u in range(2)]
        tp = ph.ps("tp", [P, kc, P])
        lp = ph.ps("lp", [P, 512])
        nb = -(-f // 512)
        fw = min(f, 512)
        fp = [ph.ps(f"fp{b}", [P, fw]) for b in range(nb)]
        wsem, step, folded = sem("weights"), sem("step"), sem("folded")
        rows_ready, rows_turned, turned_ready = sem("rows_ready"), sem("rows_turned"), sem("turned_ready")
        logits_done, feats_done, logits_free, feats_free = sem("logits_done"), sem("feats_done"), sem("logits_free"), sem("feats_free")
        staged_l, staged_f = sem("staged_l"), sem("staged_f")
        stored = [sem(f"stored{u}") for u in range(2)]
        stage_free = sem("stage_free")
        ex = extra(ph)
        block = ph.block()
        nload = len(wload(w)) + len(attload(att_b)) + len(ex.loads)

        @block.sync
        def _(sp):
            n = 0
            for out, src in wload(w) + attload(att_b):
                with nc.allow_non_contiguous_dma(reason="weights"):
                    sp.dma_start(out, src).then_inc(wsem, 16)
                n += 1
            for out, src in ex.loads:
                sp.dma_start(out, src).then_inc(wsem, 16)
                n += 1
            assert n == nload
            with sp.Fori(0, T // 2) as i:
                for u in range(2):
                    t = i * 2 + u
                    sp.wait_ge(staged_l, t + 1)
                    sp.dma_start(tabs[ds(t * P, P), :], lstage[u][:, 0:heads]).then_inc(stored[u], 16)
                    sp.dma_start(tabd[ds(t * P, P), :], lstage[u][:, heads:heads + tabd.shape[1]]).then_inc(stored[u], 16)
                    sp.wait_ge(staged_f, (t + 1) * nb)
                    sp.dma_start(table[ds(t * P, P), :], stage[u][:, :]).then_inc(stored[u], 16)
                    sp.wait_ge(stored[u], i * 48 + 48)
                    sp.sem_inc(stage_free, 1)

        @block.gpsimd
        def _(pool):
            with pool.Fori(0, T // 2) as i:
                for u in range(2):
                    ex.load(pool, i, u)

        @block.vector
        def _(dve):
            link = Steps(dve, step)
            dve.wait_ge(wsem, 16 * nload)
            for k in range(kc):
                for s in range(2):
                    link(nc.vector.tensor_tensor(prod[:, :], w[:, k, :], att_b[:, s, :], ALU.mult))
                    link(nc.vector.tensor_reduce(wa[:, k, s * heads:(s + 1) * heads],
                                                 prod[:, :].rearrange("p (h d) -> p h d", d=hw), AX_X, ALU.add))
            dve.sem_inc(folded, 1)
            dve.sem_inc(logits_free, 1)
            if hasattr(ex, "own_free"):
                dve.sem_inc(ex.own_free, 2)
            base = link.n
            per = ex.steps
            with dve.Fori(0, T // 2) as i:
                for u in range(2):
                    t = i * 2 + u
                    link = Steps(dve, step, t * per + base)
                    prep(dve, ex, link, i, u, rows[u])
                    assert link.n == per - (3 if selfloop else 1), link.n
                    dve.sem_inc(rows_ready, 1)
                    dve.wait_ge(rows_turned, t + 1)
                    nc.vector.tensor_copy(turned[u][:, :, :], tp[:, :, :]).then_inc(turned_ready, 1)
                    dve.wait_ge(logits_done, t + 1)
                    dve.wait_ge(stage_free, t + 1)
                    link(nc.vector.tensor_copy(lstage[u][:, 0:na], lp[:, 0:na]))
                    if selfloop:
                        a, b, c = (lstage[u][:, s * heads:(s + 1) * heads] for s in range(3))
                        link(nc.vector.tensor_tensor(c, a, b, ALU.add))
                        link(nc.vector.scalar_tensor_tensor(out=c, in0=c, scalar=SLOPE, in1=c, op0=ALU.mult, op1=ALU.max))
                    dve.sem_inc(staged_l, 1)
                    dve.sem_inc(logits_free, 1)

        @block.scalar
        def _(act):
            act.sem_inc(feats_free, 1)
            act.sem_inc(stage_free, 2)
            with act.Fori(0, T // 2) as i:
                for u in range(2):
                    t = i * 2 + u
                    ex.activate(act, t)
                    act.wait_ge(stage_free, t + 1)
                    for b in range(nb):
                        act.wait_ge(feats_done, t * nb + b + 1)
                        nc.scalar.copy(stage[u][:, b * fw:(b + 1) * fw], fp[b][:, :]).then_inc(staged_f, 1)
                    act.wait_ge(staged_f, (t + 1) * nb)
                    act.sem_inc(feats_free, 1)

        @block.tensor
        def _(pe):
            pe.wait_ge(folded, 1)
            with pe.Fori(0, T // 2) as i:
                for u in range(2):
                    t = i * 2 + u
                    pe.wait_ge(rows_ready, t + 1)
                    for k in range(kc):
                        ins = nc.tensor.transpose(tp[:, k, :], rows[u][:, k * P:(k + 1) * P], g.ident[:, :])
                    ins.then_inc(rows_turned, 1)
                    pe.wait_ge(turned_ready, t + 1)
                    pe.wait_ge(logits_free, t + 1)
                    for k in range(kc):
                        ins = nc.tensor.matmul(lp[:, 0:na], turned[u][:, k, :], wa[:, k, :], start=(k == 0), stop=(k == kc - 1))
                    ins.then_inc(logits_done, 1)
                    pe.wait_ge(feats_free, t + 1)
                    for b in range(nb):
                        for k in range(kc):
                            ins = nc.tensor.matmul(fp[b][:, :], turned[u][:, k, :], w[:, k, b * fw:(b + 1) * fw],
                                                   start=(k == 0), stop=(k == kc - 1))
                        ins.then_inc(feats_done, 1)


def edge_alphas(nc, g, name, heads, dwidth, selfloop, idx_s, idx_d, tabs, tabd, alpha):
    with Phase(nc, name + "_logits") as ph:
        sb, sem = ph.sb, ph.sem
        eb = sb("eb", [P, C, heads])
        esb = sb("esb", [P, C, heads]) if selfloop else None
        with ExitStack():
            rs = [sb(f"rs{u}", [P, BATCH, heads]) for u in range(2)]
            rd = [sb(f"rd{u}", [P, BATCH, dwidth]) for u in range(2)]
            cur = [sb(f"cur{u}", [P, 2, BATCH], I32) for u in range(2)]
        ea = sb("ea", [ROWS, heads, COLS])
        esa = sb("esa", [ROWS, heads, COLS]) if selfloop else None
        fw = sb("fw", [ROWS, heads, COLS])
        bw = sb("bw", [ROWS, heads, COLS])
        ends = sb("ends", [ROWS, 2, heads])
        carry = sb("carry", [ROWS, 2, heads])
        rowst = sb("rowst", [heads, 2, ROWS + 1])
        tps = [ph.ps(f"tps{j}", [P, 512]) for j in range(2)]
        ends_ps = ph.ps("ends_ps", [heads, 2, P])
        carry_ps = ph.ps("carry_ps", [ROWS, 2, heads])
        landed = ph.gathers(g, 2)
        ring_free, copied, issued, step = sem("ring_free"), sem("copied"), sem("issued"), sem("step")
        turned, untangled = sem("turned"), sem("untangled")
        ends_ready, ends_turned, rows_done, carry_turned = sem("ends_ready"), sem("ends_turned"), sem("rows_done"), sem("carry_turned")
        expin, expd, alpha_ready, aturned = sem("expin"), sem("expd"), sem("alpha_ready"), sem("aturned")
        gathered = sem("gathered")
        block = ph.block()

        @block.gpsimd
        def _(pool):
            with pool.Fori(0, CU // (2 * BATCH)) as i:
                for u in range(2):
                    n = i * 2 + u
                    pool.wait_ge(ring_free, n + 1)
                    pool.sem_inc(issued, 1)
                    for s, idx in enumerate((idx_s, idx_d)):
                        nc.gpsimd.tensor_copy(cur[u][:, s, :], idx[:, ds(n * BATCH, BATCH)]).then_inc(copied, 1)
                    pool.wait_ge(copied, (n + 1) * 2)
                    pool.sem_inc(issued, 1)
                    for b in range(BATCH):
                        nc.gpsimd.indirect_dma_start(out=rs[u][:, b, :], out_offset=None, in_=tabs,
                                                     in_offset=bass.IndirectOffsetOnAxis(ap=cur[u][:, 0, b:b + 1], axis=0)
                                                     ).then_inc(landed[u], 16)
                        nc.gpsimd.indirect_dma_start(out=rd[u][:, b, :], out_offset=None, in_=tabd,
                                                     in_offset=bass.IndirectOffsetOnAxis(ap=cur[u][:, 1, b:b + 1], axis=0)
                                                     ).then_inc(landed[u], 16)

        arrays = [(eb, ea, h) for h in range(heads)] + ([(esb, esa, h) for h in range(heads)] if selfloop else [])

        @block.tensor
        def _(pe):
            pe.wait_ge(gathered, 1)
            for j, (b, _, h) in enumerate(arrays):
                if j >= 2:
                    pe.wait_ge(untangled, j - 1)
                v = b[:, :, h].rearrange("q (r k) -> q k r", k=KB)
                for k in range(KB):
                    ins = nc.tensor.transpose(tps[j % 2][0:ROWS, k * P:(k + 1) * P], v[:, k, :], g.ident[:, :])
                ins.then_inc(turned, 1)
            for r in range(2):
                pe.wait_ge(ends_ready, r + 1)
                for s in range(2):
                    ins = nc.tensor.transpose(ends_ps[:, s, 0:ROWS], ends[:, s, :], g.ident[0:ROWS, 0:ROWS])
                ins.then_inc(ends_turned, 1)
                pe.wait_ge(rows_done, r + 1)
                nc.tensor.transpose(carry_ps[:, 0, :], rowst[:, 0, 0:ROWS], g.ident[0:heads, 0:heads])
                nc.tensor.transpose(carry_ps[:, 1, :], rowst[:, 1, 1:ROWS + 1], g.ident[0:heads, 0:heads]).then_inc(carry_turned, 1)
            for h in range(heads):
                pe.wait_ge(alpha_ready, h + 1)
                if h < 2:
                    pe.wait_ge(untangled, len(arrays))
                else:
                    pe.wait_ge(untangled, len(arrays) + h - 1)
                for k in range(KB):
                    ins = nc.tensor.transpose(tps[h % 2][:, k * P:k * P + ROWS], ea[:, h, k * P:(k + 1) * P], g.ident[0:ROWS, 0:ROWS])
                ins.then_inc(aturned, 1)

        @block.scalar
        def _(act):
            act.wait_ge(expin, 1)
            nc.scalar.activation(ea[:, :, :], ea[:, :, :], ACT.Exp).then_inc(expd, 1)
            if selfloop:
                nc.scalar.activation(esa[:, :, :], esa[:, :, :], ACT.Exp).then_inc(expd, 1)

        @block.vector
        def _(dve):
            link0 = Steps(dve, step)
            link0(nc.vector.memset(eb[:, CU:C, :], 0.0))
            if selfloop:
                link0(nc.vector.memset(esb[:, CU:C, :], 0.0))
            dve.sem_inc(ring_free, 2)
            per = 2 if selfloop else 1
            with dve.Fori(0, CU // (2 * BATCH)) as i:
                for u in range(2):
                    n = i * 2 + u
                    link = Steps(dve, step, n * per + link0.n)
                    dve.wait_ge(landed[u], (i + 1) * (16 * 2 * BATCH))
                    link(nc.vector.tensor_tensor(eb[:, ds(n * BATCH, BATCH), :], rs[u][:, :, :], rd[u][:, :, 0:heads], ALU.add))
                    if selfloop:
                        link(nc.vector.tensor_copy(esb[:, ds(n * BATCH, BATCH), :], rd[u][:, :, heads:dwidth]))
                    dve.sem_inc(ring_free, 1)
            dve.sem_inc(gathered, 1)
            link = Steps(dve, step, link0.n + per * (CU // BATCH))
            for j, (b, a, h) in enumerate(arrays):
                dve.wait_ge(turned, j + 1)
                nc.vector.tensor_copy(a[:, h, :], tps[j % 2][0:ROWS, :]).then_inc(untangled, 1)
            dve.wait_ge(untangled, len(arrays))
            link(nc.vector.scalar_tensor_tensor(out=ea[:, :, :], in0=ea[:, :, :], scalar=SLOPE, in1=ea[:, :, :],
                                                op0=ALU.mult, op1=ALU.max))

            def scans(gaps, rowgaps, op0, op1, start, rnd):
                ahead, back = gaps[:, 0:COLS], gaps[:, COLS:0:-1]

                def both(init):
                    for h in range(heads):
                        nc.vector.tensor_tensor_scan(fw[:, h, :], ahead, ea[:, h, :], init(0, h), op0, op1).then_inc(step, 1)
                        nc.vector.tensor_tensor_scan(bw[:, h, ::-1], back, ea[:, h, ::-1], init(1, h), op0, op1).then_inc(step, 1)
                        link.n += 2
                    dve.wait_ge(step, link.base + link.n)

                both(lambda s, h: start)
                link(nc.vector.tensor_copy(ends[:, 0, :], fw[:, :, COLS - 1]))
                link(nc.vector.tensor_copy(ends[:, 1, :], bw[:, :, 0]))
                dve.sem_inc(ends_ready, 1)
                link(nc.vector.memset(rowst[:, :, :], start))
                dve.wait_ge(ends_turned, rnd + 1)
                link(nc.vector.tensor_tensor_scan(rowst[:, 0, 1:ROWS + 1], rowgaps[0:heads, 0, :], ends_ps[:, 0, 0:ROWS], start, op0, op1))
                link(nc.vector.tensor_tensor_scan(rowst[:, 1, ROWS - 1::-1], rowgaps[0:heads, 1, ::-1],
                                                  ends_ps[:, 1, ROWS - 1::-1], start, op0, op1))
                dve.sem_inc(rows_done, 1)
                dve.wait_ge(carry_turned, rnd + 1)
                link(nc.vector.tensor_copy(carry[:, :, :], carry_ps[:, :, :]))
                both(lambda s, h: carry[:, s, h:h + 1])

            scans(g.apart, g.rowapart, ALU.add, ALU.max, -FAR, 0)
            link(nc.vector.tensor_tensor(fw[:, :, :], fw[:, :, :], bw[:, :, :], ALU.max))
            if selfloop:
                link(nc.vector.tensor_tensor(fw[:, :, :], fw[:, :, :], esa[:, :, :], ALU.max))
                link(nc.vector.tensor_tensor(esa[:, :, :], esa[:, :, :], fw[:, :, :], ALU.subtract))
            link(nc.vector.tensor_tensor(ea[:, :, :], ea[:, :, :], fw[:, :, :], ALU.subtract))
            dve.sem_inc(expin, 1)
            dve.wait_ge(expd, 2 if selfloop else 1)
            scans(g.same, g.rowsame, ALU.mult, ALU.add, 0.0, 1)
            link(nc.vector.tensor_tensor(fw[:, :, :], fw[:, :, :], bw[:, :, :], ALU.add))
            link(nc.vector.tensor_tensor(fw[:, :, :], fw[:, :, :], ea[:, :, :], ALU.subtract))
            if selfloop:
                link(nc.vector.tensor_tensor(fw[:, :, :], fw[:, :, :], esa[:, :, :], ALU.add))
            link(nc.vector.reciprocal(bw[:, :, :], fw[:, :, :]))
            for h in range(heads):
                nc.vector.tensor_tensor(ea[:, h, :], ea[:, h, :], bw[:, h, :], ALU.mult).then_inc(alpha_ready, 1)
            for h in range(heads):
                dve.wait_ge(aturned, h + 1)
                nc.vector.tensor_copy(alpha[:, :, h].rearrange("q (r k) -> q k r", k=KB),
                                      tps[h % 2][:, :].rearrange("q (k r) -> q k r", k=KB)[:, :, 0:ROWS]).then_inc(untangled, 1)
            dve.wait_ge(untangled, len(arrays) + heads)


def edge_messages(nc, g, name, heads, f, selfloop, idx, table, alpha, acc):
    na = heads if selfloop else 0
    hw = f // heads
    with Phase(nc, name + "_messages") as ph:
        sb, sem = ph.sb, ph.sem
        ring = [sb(f"ring{u}", [P, G, f]) for u in range(U)]
        cur = [sb(f"cur{u}", [P, G], I32) for u in range(U)]
        onehot = [sb(f"onehot{u}", [P, G, P]) for u in range(2)]
        msg = [sb(f"msg{u}", [P, G, f]) for u in range(2)]
        mp = [ph.ps(f"mp{u}", [P, 1024 if na + f > 512 else 512]) for u in range(2)]
        landed = ph.gathers(g, U)
        indexed, issued, placed = sem("indexed"), sem("issued"), sem("placed")
        cleared, onehot_made, weighted, summed, added = (sem(s) for s in ("cleared", "onehot_made", "weighted", "summed", "added"))
        block = ph.block()

        def steps(engine, i):
            regs = [engine.alloc_register(f"{name}_walk{r}") for r in range(2 * U)]
            engine.load(regs, g.walk[0:1, ds(i * U, U), :].rearrange("p s a -> p (s a)"))
            return [(engine.snap(regs[2 * u], min_val=0, max_val=CG - 1), engine.snap(regs[2 * u + 1], min_val=0, max_val=T - 1))
                    for u in range(U)]

        @block.scalar
        def _(act):
            with act.Fori(0, STEPS // U) as i:
                walk = steps(act, i)
                for u in range(U):
                    n, (c, _) = i * U + u, walk[u]
                    act.wait_ge(weighted, n + 1)
                    act.sem_inc(placed, 1)
                    nc.scalar.copy(cur[u][:, :], idx[:, ds(c * G, G)]).then_inc(indexed, 1)

        @block.gpsimd
        def _(pool):
            with pool.Fori(0, STEPS // U) as i:
                for u in range(U):
                    n = i * U + u
                    pool.wait_ge(indexed, n + 1)
                    pool.sem_inc(issued, 1)
                    for b in range(G):
                        nc.gpsimd.indirect_dma_start(out=ring[u][:, b, :], out_offset=None, in_=table,
                                                     in_offset=bass.IndirectOffsetOnAxis(ap=cur[u][:, b:b + 1], axis=0)
                                                     ).then_inc(landed[u], 16)

        @block.vector
        def _(dve):
            nc.vector.memset(acc[:, :, :], 0.0).then_inc(cleared, 1)
            dve.wait_ge(cleared, 1)
            dve.sem_inc(weighted, U)
            dve.sem_inc(summed, 2)
            dve.sem_inc(added, 2)

            def make(n, u, i, c, t):
                dve.wait_ge(summed, n + 1)
                nc.vector.tensor_tensor(onehot[u % 2][:, :, :],
                                        g.nodes[:, ds(t * P, P)].rearrange("p (b n) -> p b n", b=1).to_broadcast([P, G, P]),
                                        g.dstb[:, ds(c * G, G)].rearrange("p (b n) -> p b n", n=1).to_broadcast([P, G, P]),
                                        ALU.is_equal).then_inc(onehot_made, 1)
                dve.wait_ge(landed[u], (i + 1) * (16 * G))
                nc.vector.tensor_tensor(msg[u % 2][:, :, :].rearrange("p b (h d) -> p (b h) d", d=hw),
                                        ring[u][:, :, :].rearrange("p b (h d) -> p (b h) d", d=hw),
                                        alpha[:, ds(c * G, G), :].rearrange("p b h -> p (b h)")
                                        .rearrange("p (a d) -> p a d", d=1).to_broadcast([P, G * heads, hw]),
                                        ALU.mult).then_inc(weighted, 1)

            def add(n, u, t):
                dve.wait_ge(summed, n + 3)
                dve.wait_ge(added, n + 2)
                row = acc[:, ds(t, 1), :].rearrange("p a f -> p (a f)")
                nc.vector.tensor_tensor(row, row, mp[u % 2][:, 0:f + na], ALU.add).then_inc(added, 1)

            with dve.Fori(0, STEPS // U) as i:
                walk = steps(dve, i)
                for u in range(U):
                    n, (c, t) = i * U + u, walk[u]
                    make(n, u, i, c, t)
                    if u:
                        add(n - 1, u - 1, walk[u - 1][1])
                add(n, U - 1, t)
            dve.wait_ge(added, STEPS + 2)

        @block.tensor
        def _(pe):
            with pe.Fori(0, STEPS // U) as i:
                walk = steps(pe, i) if na else None
                for u in range(U):
                    n = i * U + u
                    pe.wait_ge(onehot_made, n + 1)
                    pe.wait_ge(weighted, n + (U + 1))
                    pe.wait_ge(added, n + 1)
                    for b in range(G):
                        ins = nc.tensor.matmul(mp[u % 2][:, 0:f], onehot[u % 2][:, b, :], msg[u % 2][:, b, :],
                                               start=(b == 0), stop=(b == G - 1))
                    if na:
                        c = walk[u][0]
                        for b in range(G):
                            ins = nc.tensor.matmul(mp[u % 2][:, f:f + na], onehot[u % 2][:, b, :],
                                                   alpha[:, ds(c * G + b, 1), :].rearrange("p a h -> p (a h)"),
                                                   start=(b == 0), stop=(b == G - 1))
                    ins.then_inc(summed, 1)


class PlainTile:

    def __init__(self, ph, steps, consts=()):
        self.steps = steps
        self.tiles = [ph.sb(f"const{n}", [P, c.shape[0]]) for n, c in enumerate(consts)]
        self.loads = [(t[:, :], row_of(c)) for t, c in zip(self.tiles, consts)]

    def load(self, pool, i, u):
        pass

    def activate(self, act, t):
        pass


class LoadedTile(PlainTile):

    def __init__(self, ph, g, steps, consts, table):
        super().__init__(ph, steps, consts)
        width = table.shape[1]
        self.table = table
        self.own = [ph.sb(f"own{u}", [P, width]) for u in range(2)]
        self.aself = ph.sb("aself", [P, 8])
        self.neg = ph.sb("neg", [P, width])
        self.landed = ph.gathers(g, 2)
        self.neg_ready, self.exp_done, self.own_free = ph.sem("neg_ready"), ph.sem("exp_done"), ph.sem("own_free")

    def load(self, pool, i, u):
        t = i * 2 + u
        pool.wait_ge(self.own_free, t + 1)
        pool.dma_start(self.own[u][:, :], self.table[ds(t * P, P), :]).then_inc(self.landed[u], 16)

    def activate(self, act, t):
        act.wait_ge(self.neg_ready, t + 1)
        act.activation(self.neg[:, :], self.neg[:, :], ACT.Exp).then_inc(self.exp_done, 1)


def add_self_loop(nc, link, ex, out, own, acc, heads, f):
    hw = f // heads
    link(nc.vector.tensor_scalar(ex.aself[:, 0:heads], acc[:, f:f + heads], -1.0, 1.0, ALU.mult, ALU.add))
    link(nc.vector.tensor_tensor(own.rearrange("p (h d) -> p h d", d=hw), own.rearrange("p (h d) -> p h d", d=hw),
                                 ex.aself[:, 0:heads].rearrange("p (h a) -> p h a", a=1).to_broadcast([P, heads, hw]), ALU.mult))
    link(nc.vector.tensor_tensor(out, own, acc[:, 0:f], ALU.add))


def route(nc, g, name, prep, prep_steps, ex_make, wr, bo, top2, xt, wts):
    with Phase(nc, name + "_route") as ph:
        sb, sem = ph.sb, ph.sem
        wr_s = sb("wr", [P, 2, R])
        bo_s = sb("bo", [R, D])
        rows = sb("rows", [P, D])
        mv = sb("mv", [P, 4])
        lg, top, topf, topi = sb("lg", [P, R]), sb("top", [P, R]), sb("topf", [P, R]), sb("topi", [P, R], U32)
        dx, one, two, wt = sb("dx", [P, R]), sb("one", [P, R]), sb("two", [P, R]), sb("wt", [P, R])
        wtt = sb("wtt", [R, P])
        tcopy = sb("tcopy", [P, 2, P])
        tp, lp, wp, bp = ph.ps("tp", [P, 2, P]), ph.ps("lp", [P, 512]), ph.ps("wp", [R, P]), ph.ps("bp", [P, 512])
        wsem, step, logits_seen = sem("weights"), sem("step"), sem("logits_seen")
        rows_ready, rows_turned, xt_ready, logits_done = sem("rows_ready"), sem("rows_turned"), sem("xt_ready"), sem("logits_done")
        dx_ready, dx_exp, wt_ready, wt_turned, wtt_ready, bias_done = (
            sem(s) for s in ("dx_ready", "dx_exp", "wt_ready", "wt_turned", "wtt_ready", "bias_done"))
        ex = ex_make(ph)
        block = ph.block()
        nload = 2 + len(ex.loads)
        tail = (11 if top2 else 6) + 3
        per = prep_steps + 1 + tail

        @block.sync
        def _(sp):
            with nc.allow_non_contiguous_dma(reason="a small matrix of weights"):
                sp.dma_start(wr_s[:, :, :], wr.rearrange("(k p) e -> p k e", p=P)).then_inc(wsem, 16)
            sp.dma_start(bo_s[:, :], bo).then_inc(wsem, 16)
            for out, src in ex.loads:
                sp.dma_start(out, src).then_inc(wsem, 16)

        @block.scalar
        def _(act):
            with act.Fori(0, T) as t:
                act.wait_ge(dx_ready, t + 1)
                nc.scalar.activation(dx[:, :], dx[:, :], ACT.Exp).then_inc(dx_exp, 1)

        @block.tensor
        def _(pe):
            pe.wait_ge(wsem, 16 * nload)
            with pe.Fori(0, T) as t:
                pe.wait_ge(rows_ready, t + 1)
                for k in range(2):
                    ins = nc.tensor.transpose(tp[:, k, :], rows[:, k * P:(k + 1) * P], g.ident[:, :])
                ins.then_inc(rows_turned, 1)
                pe.wait_ge(xt_ready, t + 1)
                for k in range(2):
                    ins = nc.tensor.matmul(lp[:, 0:R], tcopy[:, k, :], wr_s[:, k, :], start=(k == 0), stop=(k == 1))
                ins.then_inc(logits_done, 1)
                pe.wait_ge(wt_ready, t + 1)
                nc.tensor.transpose(wp[:, :], wt[:, :], g.ident[:, :]).then_inc(wt_turned, 1)
                pe.wait_ge(wtt_ready, t + 1)
                nc.tensor.matmul(bp[:, 0:D], wtt[:, :], bo_s[:, :], start=True, stop=True).then_inc(bias_done, 1)

        @block.vector
        def _(dve):
            dve.wait_ge(wsem, 16 * nload)
            with dve.Fori(0, T // 2) as i:
                for u in range(2):
                    t = i * 2 + u
                    link = Steps(dve, step, t * per)
                    prep(dve, ex, link, i, u, rows)
                    assert link.n == prep_steps, link.n
                    dve.sem_inc(rows_ready, 1)
                    dve.wait_ge(rows_turned, t + 1)
                    link(nc.vector.tensor_copy(tcopy[:, :, :], tp[:, :, :]))
                    dve.sem_inc(xt_ready, 1)
                    link(nc.vector.tensor_copy(xt[:, :, ds(t * P, P)], tcopy[:, :, :]))
                    dve.wait_ge(logits_done, t + 1)
                    link(nc.vector.tensor_tensor(lg[:, :], lp[:, 0:R], ex.tiles[-1][:, :], ALU.add))
                    if top2:
                        dve.sem_inc(logits_seen, 1)
                        link(nc.vector.max(top[:, :], lg[:, :]))
                        dve.sem_inc(logits_seen, 1)
                        link(nc.vector.max_index(topi[:, :], top[:, :], lg[:, :]))
                        link(nc.vector.tensor_copy(topf[:, :], topi[:, :]))
                        link(nc.vector.tensor_tensor(dx[:, :], top[:, :], top[:, 0:1].to_broadcast([P, R]), ALU.subtract))
                        dve.sem_inc(dx_ready, 1)
                        dve.wait_ge(dx_exp, t + 1)
                        link(nc.vector.tensor_scalar(mv[:, 0:1], dx[:, 1:2], 1.0, None, ALU.add))
                        link(nc.vector.reciprocal(mv[:, 1:2], mv[:, 0:1]))
                        link(nc.vector.tensor_tensor(mv[:, 2:3], dx[:, 1:2], mv[:, 1:2], ALU.mult))
                        link(nc.vector.tensor_scalar(one[:, :], g.nodes[:, 0:R], topf[:, 0:1], mv[:, 1:2], ALU.is_equal, ALU.mult))
                        link(nc.vector.tensor_scalar(two[:, :], g.nodes[:, 0:R], topf[:, 1:2], mv[:, 2:3], ALU.is_equal, ALU.mult))
                        link(nc.vector.tensor_tensor(wt[:, :], one[:, :], two[:, :], ALU.add))
                    else:
                        link(nc.vector.tensor_reduce(mv[:, 0:1], lg[:, :], AX_X, ALU.max))
                        link(nc.vector.tensor_scalar(dx[:, :], lg[:, :], mv[:, 0:1], None, ALU.subtract))
                        dve.sem_inc(dx_ready, 1)
                        dve.wait_ge(dx_exp, t + 1)
                        link(nc.vector.tensor_reduce(mv[:, 1:2], dx[:, :], AX_X, ALU.add))
                        link(nc.vector.reciprocal(mv[:, 2:3], mv[:, 1:2]))
                        link(nc.vector.tensor_scalar(wt[:, :], dx[:, :], mv[:, 2:3], None, ALU.mult))
                    dve.sem_inc(wt_ready, 1)
                    link(nc.vector.tensor_copy(wts[:, :, ds(t, 1)], wt[:, :].rearrange("p (e a) -> p e a", a=1)))
                    dve.wait_ge(wt_turned, t + 1)
                    nc.vector.tensor_copy(wtt[:, :], wp[:, :]).then_inc(wtt_ready, 1)
                    dve.wait_ge(bias_done, t + 1)
                    xrow = g.x[:, ds(t, 1), :].rearrange("p a f -> p (a f)")
                    link(nc.vector.tensor_tensor(xrow, xrow, bp[:, 0:D], ALU.add))
                    assert link.n == per, (link.n, per)


CT = 3
CN = CT * P
NB = T // CT // 2


def experts(nc, g, name, layers, loads, affine, params, xt, wts):
    with Phase(nc, name + "_experts") as ph:
        sb, sem = ph.sb, ph.sem
        depth = len(layers)
        w = [[sb(f"w{u}_{l}", [P, kc, mc * P]) for l, (kc, mc) in enumerate(layers)] for u in range(2)]
        wo = [sb(f"wo{u}", [P, layers[-1][1], D]) for u in range(2)]
        hid = [[sb(f"hid{a}_{l}", [P, mc, CN]) for l, (kc, mc) in enumerate(layers)] for a in range(2)]
        ncol = sum(mc for _, mc in layers)
        slot = sb("slot", [P, 2, 2, ncol])
        table = sb("table", [P, 2, R, ncol])
        up = [ph.ps(f"up{b}", [P, 512]) for b in range(4)]
        yp = [ph.ps(f"yp{b}", [P, 512]) for b in range(CT)]
        wsem = [sem(f"weights{u}") for u in range(2)]
        expert_free, up_done, act_done, y_done, y_added = (
            sem(s) for s in ("expert_free", "up_done", "act_done", "y_done", "y_added"))
        params_ready, slotted, expert_begun = sem("params_ready"), sem("slotted"), sem("expert_begun")
        pz = params.start(ph, table, params_ready)
        groups = 2 * ncol
        assert groups == 8
        block = ph.block()

        @block.sync
        def _(sp):
            params.sync(sp, pz)
            with sp.Fori(0, R // 2) as i:
                for u in range(2):
                    e = i * 2 + u
                    sp.wait_ge(expert_free, e + 1)
                    for l in range(depth):
                        sp.dma_start(w[u][l][:, :, :], loads[l][ds(e, 1), :, :].rearrange("a (k p) f -> p (a k) f", p=P)).then_inc(wsem[u], 16)
                    sp.dma_start(wo[u][:, :, :], loads[depth][ds(e, 1), :, :].rearrange("a (k p) f -> p (a k) f", p=P)).then_inc(wsem[u], 16)

        @block.tensor
        def _(pe):
            params.tensor(pe, pz)
            pe.sem_inc(expert_free, 2)
            pe.sem_inc(y_done, 2 * CT)
            with pe.Fori(0, R // 2) as i:
                for u in range(2):
                    e = i * 2 + u
                    pe.wait_ge(wsem[u], (i + 1) * (16 * (depth + 1)))
                    pe.sem_inc(expert_begun, 1)
                    with pe.Fori(0, NB) as c:
                        q = e * NB + c
                        n = 0
                        for l, (kc, mc) in enumerate(layers):
                            for a in range(2):
                                if l:
                                    pe.wait_ge(act_done, q * groups + (4 + before + (a + 1) * kc))
                                for m in range(mc):
                                    pe.wait_ge(act_done, q * groups + (n + 1))
                                    for k in range(kc):
                                        rhs = hid[a][l - 1][:, k, :] if l else xt[:, k, ds((c * 2 + a) * CN, CN)]
                                        ins = nc.tensor.matmul(up[n % 4][:, 0:CN], w[u][l][:, k, m * P:(m + 1) * P], rhs,
                                                               start=(k == 0), stop=(k == kc - 1))
                                    ins.then_inc(up_done, 1)
                                    n += 1
                            before = n - 2 * mc
                        mc = layers[-1][1]
                        for a in range(2):
                            pe.wait_ge(act_done, q * groups + (4 + before + (a + 1) * mc))
                            for j in range(CT):
                                pe.wait_ge(y_added, q * (2 * CT) + (a * CT + j + 1))
                                for k in range(mc):
                                    ins = nc.tensor.matmul(yp[j][:, 0:D], hid[a][-1][:, k, j * P:(j + 1) * P], wo[u][:, k, :],
                                                           start=(k == 0), stop=(k == mc - 1))
                                ins.then_inc(y_done, 1)
                    pe.wait_ge(y_done, (e + 1) * (NB * 2 * CT) + 2 * CT)
                    pe.sem_inc(expert_free, 1)

        @block.scalar
        def _(act):
            act.sem_inc(act_done, 4)
            params.scalar(act, pz)
            act.wait_ge(params_ready, params.ready)
            with act.Fori(0, R // 2) as i:
                for u in range(2):
                    e = i * 2 + u
                    nc.scalar.copy(slot[:, u, :, :], table[:, :, ds(e, 1), :].rearrange("p s a c -> p s (a c)")).then_inc(slotted, 1)
                    act.wait_ge(slotted, e + 1)
                    with act.Fori(0, NB) as c:
                        q = e * NB + c
                        n = col = 0
                        for l, (kc, mc) in enumerate(layers):
                            for a in range(2):
                                act.wait_ge(y_done, q * (2 * CT) + (a + 1) * CT)
                                for m in range(mc):
                                    act.wait_ge(up_done, q * groups + (n + 1))
                                    if affine:
                                        nc.scalar.activation(hid[a][l][:, m, :], up[n % 4][:, 0:CN], ACT.Relu,
                                                             bias=slot[:, u, 0, col + m:col + m + 1],
                                                             scale=slot[:, u, 1, col + m:col + m + 1]).then_inc(act_done, 1)
                                    else:
                                        nc.scalar.activation(hid[a][l][:, m, :], up[n % 4][:, 0:CN], ACT.Gelu,
                                                             bias=slot[:, u, 0, col + m:col + m + 1]).then_inc(act_done, 1)
                                    n += 1
                            col += mc

        @block.vector
        def _(dve):
            params.vector(dve, pz)
            dve.sem_inc(y_added, CT)
            with dve.Fori(0, R) as e:
                with dve.Fori(0, NB) as c:
                    for n in range(2 * CT):
                        k = (e * NB + c) * (2 * CT) + n
                        t = c * (2 * CT) + n
                        dve.wait_ge(y_done, k + (2 * CT + 1))
                        dve.wait_ge(y_added, k + CT)
                        xrow = g.x[:, ds(t, 1), :].rearrange("p a f -> p (a f)")
                        nc.vector.scalar_tensor_tensor(out=xrow, in0=yp[n % CT][:, 0:D],
                                                       scalar=wts[:, ds(e, 1), ds(t, 1)].rearrange("p a b -> p (a b)"),
                                                       in1=xrow, op0=ALU.mult, op1=ALU.add).then_inc(y_added, 1)
            dve.wait_ge(y_added, R * NB * 2 * CT + CT)


class GeluParams:

    ready = 1

    def __init__(self, nc, g, b1):
        self.nc, self.g, self.b1 = nc, g, b1

    def start(self, ph, table, ready):
        m = self.b1.shape[1] // P
        self.m, self.table, self.done = m, table, ready
        return {"raw": ph.sb("raw", [R * m, P]), "tp": ph.ps("ptp", [P, 512]),
                "loaded": ph.sem("p_loaded"), "turned": ph.sem("p_turned")}

    def scalar(self, act, z):
        pass

    def sync(self, sp, z):
        sp.dma_start(z["raw"][:, :], self.b1.rearrange("e (m p) -> (e m) p", p=P)).then_inc(z["loaded"], 16)

    def tensor(self, pe, z):
        pe.wait_ge(z["loaded"], 16)
        n = R * self.m
        pe.transpose(z["tp"][:, 0:n], z["raw"][:, :], self.g.ident[0:n, 0:n]).then_inc(z["turned"], 1)

    def vector(self, dve, z):
        dve.wait_ge(z["turned"], 1)
        self.nc.vector.memset(self.table[:, 1, :, :], 1.0).then_inc(z["turned"], 1)
        dve.wait_ge(z["turned"], 2)
        self.nc.vector.tensor_copy(self.table[:, 0, :, :], z["tp"][:, 0:R * self.m].rearrange("p (e m) -> p e m", m=self.m)
                                   ).then_inc(self.done, 1)


class NormParams:

    ready = 4
    EPS = 1e-3

    def __init__(self, nc, g, layers):
        self.nc, self.g, self.layers = nc, g, layers

    def start(self, ph, table, ready):
        self.table, self.done = table, ready
        n = R * 2
        return {"raw": [[ph.sb(f"raw{l}_{s}", [n, P]) for s in range(5)] for l in range(2)],
                "tp": ph.ps("ptp", [P, 4, R * 2]), "loaded": ph.sem("p_loaded"), "turned": ph.sem("p_turned"),
                "step": ph.sem("p_step"), "ready": ph.sem("p_ready"),
                "var_ready": ph.sem("p_var_ready"), "rooted": ph.sem("p_rooted")}

    def scalar(self, act, z):
        for l in range(2):
            act.wait_ge(z["var_ready"], l + 1)
            v = z["raw"][l][4]
            act.activation(v[:, :], v[:, :], ACT.Sqrt).then_inc(z["rooted"], 1)

    def sync(self, sp, z):
        for l in range(2):
            for tile, vec in zip(z["raw"][l], self.layers[l]):
                sp.dma_start(tile[:, :], vec.rearrange("e (m p) -> (e m) p", p=P)).then_inc(z["loaded"], 16)

    def vector(self, dve, z):
        nc, link = self.nc, Steps(dve, z["step"])
        dve.wait_ge(z["loaded"], 160)
        for l in range(2):
            b, gm, be, m, v = (t[:, :] for t in z["raw"][l])
            link(nc.vector.tensor_scalar(v, v, self.EPS, None, ALU.add))
            dve.sem_inc(z["var_ready"], 1)
            dve.wait_ge(z["rooted"], l + 1)
            link(nc.vector.reciprocal(v, v))
            link(nc.vector.tensor_tensor(gm, gm, v, ALU.mult))
            link(nc.vector.tensor_tensor(b, b, m, ALU.subtract))
            link(nc.vector.tensor_tensor(b, b, gm, ALU.mult))
            link(nc.vector.tensor_tensor(b, b, be, ALU.add))
        dve.sem_inc(z["ready"], 1)
        dve.wait_ge(z["turned"], 1)
        for l in range(2):
            for s in range(2):
                nc.vector.tensor_copy(self.table[:, s, :, l * 2:l * 2 + 2],
                                      z["tp"][:, l * 2 + s, :].rearrange("p (e m) -> p e m", m=2)).then_inc(self.done, 1)

    def tensor(self, pe, z):
        pe.wait_ge(z["ready"], 1)
        n = R * 2
        for l in range(2):
            for s in range(2):
                ins = pe.transpose(z["tp"][:, l * 2 + s, :], z["raw"][l][s][:, :], self.g.ident[0:n, 0:n])
        ins.then_inc(z["turned"], 1)


def store(nc, g, out):
    with Phase(nc, "store") as ph:
        stored = ph.sem("stored")
        block = ph.block()

        @block.sync
        def _(sp):
            sp.dma_start(out[0:(T - 1) * P, :].rearrange("(t p) f -> p t f", p=P), g.x[:, 0:T - 1, :]).then_inc(stored, 16)
            sp.dma_start(out[(T - 1) * P:N, :], g.x[0:LAST, T - 1, :]).then_inc(stored, 16)
            sp.wait_ge(stored, 32)


class Persistent:

    def __init__(self, ctx, nc):
        def sb(name, shape, dt=F32):
            return ctx.enter_context(nc.sbuf_tensor(name, shape, dt))

        self.ctx = ctx
        self.x = sb("x", [P, T, D])
        self.mean, self.rstd = sb("mean", [P, T]), sb("rstd", [P, T])
        self.ident = sb("ident", [P, P])
        self.nodes = sb("nodes", [P, NP])
        self.dstb = sb("dstb", [P, C])
        self.dsti, self.srci = sb("dsti", [P, C], I32), sb("srci", [P, C], I32)
        self.srct, self.dstt = sb("srct", [P, C], I32), sb("dstt", [P, C], I32)
        self.same, self.apart = sb("same", [ROWS, COLS + 1]), sb("apart", [ROWS, COLS + 1])
        self.rowsame, self.rowapart = sb("rowsame", [8, 2, ROWS]), sb("rowapart", [8, 2, ROWS])
        self.walk = sb("walk", [1, STEPS, 2], I32)


def gnn_ffn(nc, x, src, dst, edge_type_8, w, out, stop=99):
    table0 = nc.dram_tensor("table0", [NP, R * D], F32).ap()
    tabs0 = nc.dram_tensor("tabs0", [NP, R * 4], F32).ap()
    tabd0 = nc.dram_tensor("tabd0", [NP, R * 4], F32).ap()
    table1 = nc.dram_tensor("table1", [NP, 512], F32).ap()
    tabs1 = nc.dram_tensor("tabs1", [NP, 8], F32).ap()
    tabd1 = nc.dram_tensor("tabd1", [NP, 16], F32).ap()
    table2 = nc.dram_tensor("table2", [NP, D], F32).ap()
    tabs2 = nc.dram_tensor("tabs2", [NP, 1], F32).ap()
    tabd2 = nc.dram_tensor("tabd2", [NP, 2], F32).ap()
    with ExitStack() as ctx:
        g = Persistent(ctx, nc)

        def tile_of(t):
            return g.x[:, ds(t, 1), :].rearrange("p a f -> p (a f)")

        setup(nc, g, x, src, dst, edge_type_8)

        node_stats(nc, g, "p0", False)
        conv, hd = w["L0_gnn_conv_weights"], D // 4
        project(nc, g, "p0", 2, R * D, R * 4,
                lambda t: [(t[:, k, :].rearrange("p (r d) -> p r d", d=hd),
                            conv.rearrange("r h (k i) d -> k i (r h) d", i=P)[k]) for k in range(2)],
                lambda t: [(t[:, s, :], row_of(w[n].rearrange("r h d -> (r h d)"))) for s, n in enumerate(("L0_gnn_attn_l", "L0_gnn_attn_r"))],
                lambda dve, ex, link, i, u, rows: normed(nc, g, link, rows[:, :], i * 2 + u),
                table0, tabs0, tabd0, False, lambda ph: PlainTile(ph, 2))
        with ExitStack() as c0:
            acc0 = c0.enter_context(nc.sbuf_tensor("acc0", [P, T, D], F32))
            alpha0 = c0.enter_context(nc.sbuf_tensor("alpha0", [P, C, 4], F32))
            edge_alphas(nc, g, "e0", 4, 4, False, g.srct, g.dstt,
                        tabs0.rearrange("n (r h) -> (n r) h", h=4), tabd0.rearrange("n (r h) -> (n r) h", h=4), alpha0)
            edge_messages(nc, g, "e0", 4, D, False, g.srct, table0.rearrange("n (r f) -> (n r) f", f=D), alpha0, acc0)
            xt0 = c0.enter_context(nc.sbuf_tensor("xt0", [P, 2, NP], F32))
            wts0 = c0.enter_context(nc.sbuf_tensor("wts0", [P, R, T], F32))

            def prep_f0(dve, ex, link, i, u, rows):
                normed(nc, g, link, rows[:, :], i * 2 + u)
                link(nc.vector.tensor_tensor(rows[:, :], rows[:, :], ex.tiles[0][:, :], ALU.mult))
                link(nc.vector.tensor_tensor(rows[:, :], rows[:, :], ex.tiles[1][:, :], ALU.add))

            def update0(dve, link, consts):
                link(nc.vector.tensor_tensor(g.x[:, :, :], g.x[:, :, :], acc0[:, :, :], ALU.add))
                link(nc.vector.tensor_tensor(g.x[:, :, :], g.x[:, :, :], consts[0].rearrange("p (a f) -> p a f", a=1).to_broadcast([P, T, D]), ALU.add))

            node_stats(nc, g, "f0", True, alloc=lambda ph: [(ph.sb("bias", [P, D])[:, :], row_of(w["L0_gnn_h_bias"]))], update=update0)
            if stop == 0:
                store(nc, g, out)
                return
            route(nc, g, "f0", prep_f0, 3,
                  lambda ph: PlainTile(ph, 0, (w["L0_ffn_gamma"], w["L0_ffn_beta"], w["L0_ffn_br"])),
                  w["L0_ffn_Wr"], w["L0_ffn_b2"], True, xt0, wts0)
            if stop > 1:
                experts(nc, g, "f0", [(2, 4)], [w["L0_ffn_W1"], w["L0_ffn_W2"]], False, GeluParams(nc, g, w["L0_ffn_b1"]), xt0, wts0)
        if stop <= 2:
            store(nc, g, out)
            return

        def prep_p1(dve, ex, link, i, u, rows):
            normed(nc, g, link, rows[:, :], i * 2 + u)
            link(nc.vector.tensor_tensor(rows[:, :], rows[:, :], ex.tiles[0][:, :], ALU.mult))
            link(nc.vector.tensor_tensor(rows[:, :], rows[:, :], ex.tiles[1][:, :], ALU.add))

        node_stats(nc, g, "p1", True)
        project(nc, g, "p1", 2, 512, 8,
                lambda t: [(t[:, :, :], w["L1_gnn_W1"].rearrange("(k i) f -> i k f", i=P))],
                lambda t: [(t[:, s, :], row_of(w[n].rearrange("h d -> (h d)"))) for s, n in enumerate(("L1_gnn_att_src1", "L1_gnn_att_dst1"))],
                prep_p1, table1, tabs1, tabd1, True, lambda ph: PlainTile(ph, 6, (w["L1_gnn_ln_w"], w["L1_gnn_ln_b"])))
        with ExitStack() as c1:
            alpha1 = c1.enter_context(nc.sbuf_tensor("alpha1", [P, C, 8], F32))
            edge_alphas(nc, g, "e1", 8, 16, True, g.srci, g.dsti, tabs1, tabd1, alpha1)
            acc1 = c1.enter_context(nc.sbuf_tensor("acc1", [P, T, 520], F32))
            edge_messages(nc, g, "e1", 8, 512, True, g.srci, table1, alpha1, acc1)

            def prep_p2(dve, ex, link, i, u, rows):
                t = i * 2 + u
                dve.wait_ge(ex.landed[u], (i + 1) * 16)
                add_self_loop(nc, link, ex, rows[:, :], ex.own[u][:, :], acc1[:, ds(t, 1), :].rearrange("p a f -> p (a f)"), 8, 512)
                dve.sem_inc(ex.own_free, 1)
                link(nc.vector.tensor_tensor(rows[:, :], rows[:, :], ex.tiles[0][:, :], ALU.add))
                link(nc.vector.tensor_scalar(ex.neg[:, :], rows[:, :], 0.0, None, ALU.min))
                dve.sem_inc(ex.neg_ready, 1)
                link(nc.vector.tensor_scalar(rows[:, :], rows[:, :], 0.0, -1.0, ALU.max, ALU.add))
                dve.wait_ge(ex.exp_done, t + 1)
                link(nc.vector.tensor_tensor(rows[:, :], rows[:, :], ex.neg[:, :], ALU.add))

            project(nc, g, "p2", 4, D, 1,
                    lambda t: [(t[:, :, :], w["L1_gnn_W2"].rearrange("(k i) f -> i k f", i=P))],
                    lambda t: [(t[:, s, :], row_of(w[n].rearrange("h d -> (h d)"))) for s, n in enumerate(("L1_gnn_att_src2", "L1_gnn_att_dst2"))],
                    prep_p2, table2, tabs2, tabd2, True, lambda ph: LoadedTile(ph, g, 10, (w["L1_gnn_b1"],), table1))
        with ExitStack() as c2:
            alpha2 = c2.enter_context(nc.sbuf_tensor("alpha2", [P, C, 1], F32))
            acc2 = c2.enter_context(nc.sbuf_tensor("acc2", [P, T, D + 1], F32))
            edge_alphas(nc, g, "e2", 1, 2, True, g.srci, g.dsti, tabs2, tabd2, alpha2)
            edge_messages(nc, g, "e2", 1, D, True, g.srci, table2, alpha2, acc2)
            xt1 = c2.enter_context(nc.sbuf_tensor("xt1", [P, 2, NP], F32))
            wts1 = c2.enter_context(nc.sbuf_tensor("wts1", [P, R, T], F32))

            def update1(dve, link, tiles):
                own, bias = tiles
                aself = wts1[:, 0, :].rearrange("p (t a) -> p t a", a=1)
                link(nc.vector.tensor_scalar(aself, acc2[:, :, D:D + 1], -1.0, 1.0, ALU.mult, ALU.add))
                link(nc.vector.tensor_tensor(own, own, aself.to_broadcast([P, T, D]), ALU.mult))
                for more in (own, acc2[:, :, 0:D], bias.rearrange("p (a f) -> p a f", a=1).to_broadcast([P, T, D])):
                    link(nc.vector.tensor_tensor(g.x[:, :, :], g.x[:, :, :], more, ALU.add))

            node_stats(nc, g, "f1", False, update=update1,
                       alloc=lambda ph: [(ph.sb("own", [P, T, D])[:, :, :], table2.rearrange("(t p) f -> p t f", p=P)),
                                         (ph.sb("bias", [P, D])[:, :], row_of(w["L1_gnn_b2"]))])
            route(nc, g, "f1", lambda dve, ex, link, i, u, rows: normed(nc, g, link, rows[:, :], i * 2 + u), 1,
                  lambda ph: PlainTile(ph, 0, (w["L1_ffn_br"],)),
                  w["L1_ffn_Wr"], w["L1_ffn_bo"], False, xt1, wts1)
            p = {k: w[f"L1_ffn_{k}"] for k in ("b1", "g1", "be1", "m1", "v1", "b2", "g2", "be2", "m2", "v2")}
            experts(nc, g, "f1", [(2, 2), (2, 2)], [w["L1_ffn_W1"], w["L1_ffn_W2"], w["L1_ffn_Wo"]], True,
                    NormParams(nc, g, [[p[k + str(l)] for k in ("b", "g", "be", "m", "v")] for l in (1, 2)]), xt1, wts1)
        store(nc, g, out)


_INS = ["x", "src", "dst", "edge_type_8"]
_WEIGHTS = ["L0_gnn_conv_weights", "L0_gnn_attn_l", "L0_gnn_attn_r", "L0_gnn_h_bias", "L0_ffn_gamma", "L0_ffn_beta",
            "L0_ffn_Wr", "L0_ffn_br", "L0_ffn_W1", "L0_ffn_b1", "L0_ffn_W2", "L0_ffn_b2", "L1_gnn_ln_w", "L1_gnn_ln_b",
            "L1_gnn_W1", "L1_gnn_att_src1", "L1_gnn_att_dst1", "L1_gnn_b1", "L1_gnn_W2", "L1_gnn_att_src2",
            "L1_gnn_att_dst2", "L1_gnn_b2", "L1_ffn_Wr", "L1_ffn_br", "L1_ffn_W1", "L1_ffn_b1", "L1_ffn_g1", "L1_ffn_be1",
            "L1_ffn_m1", "L1_ffn_v1", "L1_ffn_W2", "L1_ffn_b2", "L1_ffn_g2", "L1_ffn_be2", "L1_ffn_m2", "L1_ffn_v2",
            "L1_ffn_Wo", "L1_ffn_bo"]


def kernel(**inputs):
    import numpy as _np
    import concourse.bacc as _bacc
    from concourse import mybir as _mybir
    from concourse.bass_utils import run_bass_kernel_spmd as _run

    nc = _bacc.Bacc("TRN2", target_bir_lowering=False, num_devices=1)
    arrays, args = {}, {}
    for name in _INS + _WEIGHTS:
        a = _np.ascontiguousarray(inputs[name])
        arrays[f"in_{name}_dram"] = a
        args[name] = nc.dram_tensor(f"in_{name}_dram", a.shape, _mybir.dt.from_np(a.dtype), kind="ExternalInput").ap()
    out = nc.dram_tensor("out_0_dram", (N, D), _mybir.dt.float32, kind="ExternalOutput").ap()
    gnn_ffn(nc, *[args[n] for n in _INS], {n: args[n] for n in _WEIGHTS}, out, STOP)
    r = _run(nc, [arrays], core_ids=[0])
    return r.results[0]["out_0_dram"]
```

```python
from contextlib import ExitStack

import concourse.bass as bass
from concourse import mybir

F32 = mybir.dt.float32
I32 = mybir.dt.int32
BF16 = mybir.dt.bfloat16
U32 = mybir.dt.uint32
ALU = mybir.AluOpType
ACT = mybir.ActivationFunctionType
AX_X = mybir.AxisListType.X
ds = bass.ds

P = 128
N, D, E, R = 3750, 256, 60000, 8
T = -(-N // P)
NP = T * P
LAST = N - (T - 1) * P
COLS = 512
ROWS = -(-E // COLS)
TAIL = E - (ROWS - 1) * COLS
KB = COLS // P
C = ROWS * KB
G = 2
CU = -(-E // (P * G)) * G
CG = CU // G
STEPS = CG + T - 1
FAR = 1.0e30
SLOPE = 0.2
EPS = 1e-5
STOP = 99
BATCH = 5
U = 12
RING = 4
BUFS = 3
LAG = 2
LOW = 2 * P
HIGH = NP // LOW
LB = 47
assert NP % LOW == 0 and CU % LB == 0
assert CU % (2 * BATCH) == 0 and STEPS % U == 0 and U % RING == 0 and U % BUFS == 0 and T % 2 == 0


class Steps:

    def __init__(self, engine, sem, base=0):
        self.engine, self.sem, self.base, self.n = engine, sem, base, 0

    def __call__(self, ins):
        ins.then_inc(self.sem, 1)
        self.n += 1
        self.engine.wait_ge(self.sem, self.base + self.n)
        return ins


class Phase:

    def __init__(self, nc, name):
        self.nc, self.name, self.ctx = nc, name, ExitStack()
        self.inner, self.sems = ExitStack(), []

    def __enter__(self):
        return self

    def __exit__(self, *a):
        self.inner.__exit__(*a)
        if a[0] is None:
            for s in self.sems:
                self.nc.gpsimd.sem_clear(s)
            self.nc.all_engine_barrier()
        return self.ctx.__exit__(*a)

    def sb(self, name, shape, dt=F32):
        return self.ctx.enter_context(self.nc.sbuf_tensor(f"{self.name}_{name}", shape, dt))

    def ps(self, name, shape, dt=F32):
        return self.ctx.enter_context(self.nc.psum_tensor(f"{self.name}_{name}", shape, dt))

    def sem(self, name):
        self.sems.append(self.ctx.enter_context(self.nc.semaphore(f"{self.name}_{name}")))
        return self.sems[-1]

    def gathers(self, g, n, what="landed"):
        return [g.ctx.enter_context(self.nc.semaphore(f"{self.name}_{what}{u}")) for u in range(n)]

    def block(self):
        return self.inner.enter_context(self.nc.Block())


def row_of(vector, parts=P):
    return vector.rearrange("(a d) -> a d", a=1).to_broadcast([parts, vector.shape[0]])


def normed(nc, g, link, out, t):
    link(nc.vector.tensor_scalar(out, g.x[:, ds(t, 1), :].rearrange("p a f -> p (a f)"),
                                 g.mean[:, ds(t, 1)], g.rstd[:, ds(t, 1)], ALU.subtract, ALU.mult))


def node_stats(nc, g, name, twice, loads=(), alloc=None, update=None):
    with Phase(nc, name + "_stats") as ph:
        step, loaded, var_ready, rooted = (ph.sem(s) for s in ("step", "loaded", "var_ready", "rooted"))
        raw = ph.sb("raw", [P, T, 6])
        stat = ph.sb("stat", [P, T, 2])
        root, again = ph.sb("root", [P, T]), ph.sb("again", [P, T])
        pairs = alloc(ph) if alloc else []
        block = ph.block()

        @block.sync
        def _(sp):
            for out, src in pairs:
                sp.dma_start(out, src).then_inc(loaded, 16)

        @block.vector
        def _(dve):
            link = Steps(dve, step)
            if update:
                dve.wait_ge(loaded, 16 * len(pairs))
                update(dve, link, [out for out, _ in pairs])
            base = link.n
            with dve.Fori(0, T) as t:
                nc.vector.bn_stats(raw[:, ds(t, 1), :].rearrange("p a s -> p (a s)"),
                                   g.x[:, ds(t, 1), :].rearrange("p a f -> p (a f)")).then_inc(step, 1)
            link = Steps(dve, step, base + T)
            dve.wait_ge(step, base + T)
            half, square = stat[:, :, 0], stat[:, :, 1]
            link(nc.vector.tensor_tensor(half, raw[:, :, 1], raw[:, :, 4], ALU.add))
            link(nc.vector.tensor_scalar(g.mean[:, :], half, 0.5, None, ALU.mult))
            link(nc.vector.tensor_tensor(half, raw[:, :, 1], raw[:, :, 4], ALU.subtract))
            link(nc.vector.tensor_scalar(half, half, 0.5, None, ALU.mult))
            link(nc.vector.tensor_tensor(half, half, half, ALU.mult))
            link(nc.vector.tensor_tensor(square, raw[:, :, 2], raw[:, :, 5], ALU.add))
            link(nc.vector.scalar_tensor_tensor(out=square, in0=square, scalar=1.0 / D, in1=half, op0=ALU.mult, op1=ALU.add))
            link(nc.vector.tensor_scalar(root[:, :], stat[:, :, 1], EPS, None, ALU.add))
            dve.sem_inc(var_ready, 1)
            dve.wait_ge(rooted, 1)
            link(nc.vector.reciprocal(g.rstd[:, :], root[:, :]))
            if twice:
                link(nc.vector.tensor_tensor(again[:, :], g.rstd[:, :], g.rstd[:, :], ALU.mult))
                link(nc.vector.tensor_tensor(again[:, :], again[:, :], stat[:, :, 1], ALU.mult))
                link(nc.vector.tensor_scalar(root[:, :], again[:, :], EPS, None, ALU.add))
                dve.sem_inc(var_ready, 1)
                dve.wait_ge(rooted, 2)
                link(nc.vector.reciprocal(again[:, :], root[:, :]))
                link(nc.vector.tensor_tensor(g.rstd[:, :], g.rstd[:, :], again[:, :], ALU.mult))

        @block.scalar
        def _(act):
            for r in range(2 if twice else 1):
                act.wait_ge(var_ready, r + 1)
                nc.scalar.activation(root[:, :], root[:, :], ACT.Sqrt).then_inc(rooted, 1)


def setup(nc, g, x, src, dst, etype, src_low):
    with Phase(nc, "setup") as ph:
        sb, sem = ph.sb, ph.sem
        dstx = sb("dstx", [ROWS, COLS + 2], I32)
        srca = sb("srca", [ROWS, COLS], I32)
        typa = sb("typa", [ROWS, COLS], I32)
        fa = sb("fa", [ROWS, 3, COLS])
        dstf = sb("dstf", [ROWS, COLS + 2])
        rowc = sb("rowc", [ROWS, 2, 8])
        tli = sb("tli", [ROWS, KB // G], I32)
        key = sb("key", [ROWS, KB // G])
        cmp = sb("cmp", [ROWS, KB // G, STEPS])
        ones = sb("ones", [P, 1])
        tps = [ph.ps(f"tps{a}", [P, KB, P]) for a in range(3)]
        rps = ph.ps("rps", [8, 2, P])
        cps = ph.ps("cps", [1, 512])
        bits = sb("bits", [ROWS, COLS], I32)
        low = sb("low", [ROWS, COLS], BF16)
        filled, loaded, xloaded = sem("filled"), sem("loaded"), sem("xloaded")
        made, step, fready, turned = sem("made"), sem("step"), sem("fready"), sem("turned")
        identr, cmpr, counted = sem("identr"), sem("cmpr"), sem("counted")
        low_ready, kept = sem("low_ready"), sem("kept")
        block = ph.block()

        @block.sync
        def _(sp):
            sp.dma_start(g.x[:, 0:T - 1, :], x[0:(T - 1) * P, :].rearrange("(t p) f -> p t f", p=P)).then_inc(xloaded, 16)
            sp.wait_ge(filled, 4)
            sp.dma_start(g.x[0:LAST, T - 1, :], x[(T - 1) * P:N, :]).then_inc(xloaded, 16)
            full = (ROWS - 1) * COLS
            for tile, vec in ((dstx[:, 1:COLS + 1], dst), (srca[:, :], src), (typa[:, :], etype)):
                sp.dma_start(tile[0:ROWS - 1, :], vec[0:full].rearrange("(r c) -> r c", c=COLS)).then_inc(loaded, 16)
                sp.dma_start(tile[ROWS - 1:ROWS, 0:TAIL], vec[full:E].rearrange("(r c) -> r c", r=1)).then_inc(loaded, 16)
            with nc.allow_non_contiguous_dma(reason="one edge of each row"):
                sp.dma_start(dstx[1:ROWS, 0:1], dst[0:full].rearrange("(r c) -> r c", c=COLS)[:, COLS - 1:COLS]).then_inc(loaded, 16)
                sp.dma_start(dstx[0:ROWS - 2, COLS + 1:COLS + 2],
                             dst[0:full].rearrange("(r c) -> r c", c=COLS)[1:ROWS - 1, 0:1]).then_inc(loaded, 16)
                sp.dma_start(dstx[ROWS - 2:ROWS - 1, COLS + 1:COLS + 2],
                             dst[full:full + 1].rearrange("(r c) -> r c", c=1)).then_inc(loaded, 16)
            sp.wait_ge(loaded, 16 * 9)
            sp.wait_ge(xloaded, 32)
            sp.wait_ge(low_ready, 1)
            sp.dma_start(src_low.rearrange("(r c) -> r c", c=COLS), low[:, :]).then_inc(kept, 16)
            sp.wait_ge(kept, 16)

        @block.gpsimd
        def _(pool):
            nc.gpsimd.memset(g.x[:, T - 1, :], 0.0).then_inc(filled, 1)
            nc.gpsimd.memset(dstx[:, :], NP - 1).then_inc(filled, 1)
            nc.gpsimd.memset(srca[:, :], 0).then_inc(filled, 1)
            nc.gpsimd.memset(typa[:, :], 0).then_inc(filled, 1)
            nc.gpsimd.iota(g.pcol[:, :], [[0, 1]], base=0, channel_multiplier=1,
                           allow_small_or_imprecise_dtypes=True).then_inc(made, 1)
            nc.gpsimd.iota(g.nodes[:, :], [[1, NP]], base=0, channel_multiplier=0,
                           allow_small_or_imprecise_dtypes=True).then_inc(made, 1)
            nc.gpsimd.iota(key[:, :], [[1, KB // G]], base=0, channel_multiplier=KB // G,
                           allow_small_or_imprecise_dtypes=True).then_inc(made, 1)

        @block.vector
        def _(dve):
            link = Steps(dve, step)
            dve.wait_ge(made, 3)
            nc.vector.tensor_scalar(g.ident[:, :], g.nodes[:, 0:P], g.pcol[:, 0:1], None, ALU.is_equal).then_inc(identr, 1)
            link(nc.vector.memset(ones[:, :], 1.0))
            dve.wait_ge(loaded, 16 * 9)
            link(nc.vector.tensor_copy(dstf[:, :], dstx[:, :]))
            link(nc.vector.tensor_copy(g.before[:, :], dstx[:, 0:1]))
            link(nc.vector.tensor_copy(g.typr[:, :], typa[:, :]))
            link(nc.vector.tensor_scalar(bits[:, :], srca[:, :], LOW - 1, None, ALU.bitwise_and))
            link(nc.vector.tensor_copy(low[:, :], bits[:, :]))
            dve.sem_inc(low_ready, 1)
            nc.vector.tensor_copy(fa[:, 0, :], dstf[:, 1:COLS + 1]).then_inc(fready, 1)
            nc.vector.tensor_copy(fa[:, 1, :], srca[:, :]).then_inc(fready, 1)
            nc.vector.scalar_tensor_tensor(out=fa[:, 2, :], in0=srca[:, :], scalar=float(R), in1=typa[:, :],
                                           op0=ALU.mult, op1=ALU.add).then_inc(fready, 1)
            link(nc.vector.tensor_tensor(g.same[:, :], dstf[:, 0:COLS + 1], dstf[:, 1:COLS + 2], ALU.is_equal))
            link(nc.vector.tensor_scalar(g.apart[:, :], g.same[:, :], 1.0, FAR, ALU.subtract, ALU.mult))
            nc.vector.tensor_tensor(rowc[:, 0, :], dstf[:, 0:1].to_broadcast([ROWS, 8]),
                                    dstf[:, COLS:COLS + 1].to_broadcast([ROWS, 8]), ALU.is_equal).then_inc(fready, 1)
            nc.vector.tensor_tensor(rowc[:, 1, :], dstf[:, 1:2].to_broadcast([ROWS, 8]),
                                    dstf[:, COLS + 1:COLS + 2].to_broadcast([ROWS, 8]), ALU.is_equal).then_inc(fready, 1)
            link(nc.vector.tensor_scalar(tli[:, :], dstx[:, 1:COLS + 1].rearrange("r (k c) -> r k c", c=G * P)[:, :, G * P - 1],
                                         7, None, ALU.arith_shift_right))
            link(nc.vector.tensor_tensor(key[:, :], key[:, :], tli[:, :], ALU.add))
            for k in range(KB // G):
                ins = nc.vector.tensor_scalar(cmp[:, k, :], g.nodes[0:ROWS, 0:STEPS], key[:, k:k + 1], None, ALU.is_gt)
            ins.then_inc(cmpr, 1)
            outs = ((g.dstb, g.dsti), (None, g.srci), (None, g.srct))
            for a, (flt, integer) in enumerate(outs):
                dve.wait_ge(turned, a + 1)
                for out in (flt, integer):
                    if out is not None:
                        link(nc.vector.tensor_copy(out[:, :].rearrange("q (r k) -> q k r", k=KB), tps[a][:, :, 0:ROWS]))
            dve.wait_ge(turned, 4)
            link(nc.vector.tensor_copy(g.rowsame[:, :, :], rps[:, :, 0:ROWS]))
            link(nc.vector.tensor_scalar(g.rowapart[:, :, :], g.rowsame[:, :, :], 1.0, FAR, ALU.subtract, ALU.mult))
            dve.wait_ge(counted, 1)
            link(nc.vector.memset(g.walk[:, 0:LAG, :], 0))
            link(nc.vector.tensor_copy(g.walk[:, LAG:LAG + STEPS, 0], cps[0:1, 0:STEPS]))
            link(nc.vector.tensor_tensor(g.walk[:, LAG:LAG + STEPS, 1], g.nodes[0:1, 0:STEPS], cps[0:1, 0:STEPS], ALU.subtract))

        @block.tensor
        def _(pe):
            pe.wait_ge(identr, 1)
            for a in range(3):
                pe.wait_ge(fready, a + 1)
                for k in range(KB):
                    ins = nc.tensor.transpose(tps[a][:, k, 0:ROWS], fa[:, a, k * P:(k + 1) * P], g.ident[0:ROWS, 0:ROWS])
                ins.then_inc(turned, 1)
            pe.wait_ge(fready, 5)
            for a in range(2):
                ins = nc.tensor.transpose(rps[:, a, 0:ROWS], rowc[:, a, :], g.ident[0:ROWS, 0:ROWS])
            ins.then_inc(turned, 1)
            pe.wait_ge(cmpr, 1)
            for k in range(KB // G):
                ins = nc.tensor.matmul(cps[0:1, 0:STEPS], ones[0:ROWS, :], cmp[:, k, :], start=(k == 0), stop=(k == KB // G - 1))
            ins.then_inc(counted, 1)


def node_starts(nc, g, spreads):
    with Phase(nc, "starts") as ph:
        sb, sem = ph.sb, ph.sem
        zeros = sb("zeros", [ROWS, 4096])
        bits = [sb(f"bits{s}", [P, CU], I32) for s in range(2)]
        part = [sb(f"part{s}", [P, CU], BF16) for s in range(2)]
        iota = sb("iota", [P, P], BF16)
        lo = [sb(f"lo{u}", [P, LB, P], BF16) for u in range(2)]
        hi = [sb(f"hi{u}", [P, LB, T], BF16) for u in range(2)]
        hist, less, ones = sb("hist", [P, T]), sb("less", [P, P]), sb("ones", [P, P])
        total, upto, some, first = (sb(s, [P, T]) for s in ("total", "upto", "some", "first"))
        hp = [ph.ps(f"hp{u}", [P, 512]) for u in range(2)]
        pp = ph.ps("pp", [P, 2, 64])
        zeroed, cleared, step, onehots, counted, hist_ready, summed = (
            sem(s) for s in ("zeroed", "cleared", "step", "onehots", "counted", "hist_ready", "summed"))
        block = ph.block()
        n_zero = 0
        for spread in spreads:
            n_zero += -(-COLS * spread.shape[1] // 4096)

        @block.sync
        def _(sp):
            sp.wait_ge(cleared, 1)
            for spread in spreads:
                rows = spread[0:ROWS * COLS, :].rearrange("(r c) w -> r (c w)", c=COLS)
                for at in range(0, COLS * spread.shape[1], 4096):
                    size = min(4096, COLS * spread.shape[1] - at)
                    sp.dma_start(rows[:, at:at + size], zeros[:, 0:size]).then_inc(zeroed, 16)
            sp.wait_ge(zeroed, 16 * n_zero)

        @block.vector
        def _(dve):
            link = Steps(dve, step)
            nc.vector.memset(zeros[:, :], 0.0).then_inc(cleared, 1)
            link(nc.vector.memset(hist[:, :], 0.0))
            link(nc.vector.memset(ones[:, :], 1.0))
            link(nc.vector.tensor_copy(iota[:, :], g.nodes[:, 0:P]))
            link(nc.vector.tensor_scalar(less[:, :], g.nodes[:, 0:P], g.pcol[:, 0:1], None, ALU.is_gt))
            link(nc.vector.tensor_scalar(bits[0][:, :], g.dsti[:, 0:CU], P - 1, None, ALU.bitwise_and))
            link(nc.vector.tensor_scalar(bits[1][:, :], g.dsti[:, 0:CU], 7, None, ALU.arith_shift_right))
            for s in range(2):
                link(nc.vector.tensor_copy(part[s][:, :], bits[s][:, :]))
            for k in range(CU // LB):
                u = k % 2
                if k >= 2:
                    dve.wait_ge(counted, k - 1)
                    link(nc.vector.tensor_tensor(hist[:, :], hist[:, :], hp[u][:, 0:T], ALU.add))
                for one, s, width in ((lo[u], 0, P), (hi[u], 1, T)):
                    link(nc.vector.tensor_tensor(one[:, :, :],
                                                 iota[:, 0:width].rearrange("p (b n) -> p b n", b=1).to_broadcast([P, LB, width]),
                                                 part[s][:, k * LB:(k + 1) * LB].rearrange("p (b n) -> p b n", n=1)
                                                 .to_broadcast([P, LB, width]), ALU.is_equal))
                dve.sem_inc(onehots, 1)
            for k in range(CU // LB, CU // LB + 2):
                dve.wait_ge(counted, k - 1)
                link(nc.vector.tensor_tensor(hist[:, :], hist[:, :], hp[k % 2][:, 0:T], ALU.add))
            dve.sem_inc(hist_ready, 1)
            dve.wait_ge(summed, 1)
            link(nc.vector.tensor_copy(total[:, :], pp[:, 1, 0:T]))
            link(nc.vector.tensor_tensor_scan(upto[:, :], ones[:, 0:T], total[:, :], 0.0, ALU.mult, ALU.add))
            link(nc.vector.tensor_tensor(upto[:, :], upto[:, :], total[:, :], ALU.subtract))
            link(nc.vector.tensor_tensor(upto[:, :], upto[:, :], pp[:, 0, 0:T], ALU.add))
            link(nc.vector.tensor_scalar(some[:, :], hist[:, :], 0.0, None, ALU.is_gt))
            own = g.nodes[:, :].rearrange("p (t n) -> p t n", n=P)[:, :, 0]
            link(nc.vector.tensor_scalar(first[:, :], own, g.pcol[:, 0:1], float(ROWS * COLS), ALU.add, ALU.add))
            link(nc.vector.tensor_tensor(upto[:, :], upto[:, :], first[:, :], ALU.subtract))
            link(nc.vector.tensor_tensor(upto[:, :], upto[:, :], some[:, :], ALU.mult))
            link(nc.vector.tensor_tensor(g.first[:, :], upto[:, :], first[:, :], ALU.add))

        @block.tensor
        def _(pe):
            for k in range(CU // LB):
                u = k % 2
                pe.wait_ge(onehots, k + 1)
                for b in range(LB):
                    ins = nc.tensor.matmul(hp[u][:, 0:T], lo[u][:, b, :], hi[u][:, b, :], start=(b == 0), stop=(b == LB - 1))
                ins.then_inc(counted, 1)
            pe.wait_ge(hist_ready, 1)
            nc.tensor.matmul(pp[:, 0, 0:T], less[:, :], hist[:, :], start=True, stop=True)
            nc.tensor.matmul(pp[:, 1, 0:T], ones[:, :], hist[:, :], start=True, stop=True).then_inc(summed, 1)


def project(nc, g, name, kc, f, heads, w, wload, attload, prep, features, table, tabs, tabd, xt, selfloop, extra):
    hw = f // heads
    na = 2 * heads
    keep = xt is not None
    with Phase(nc, name) as ph:
        sb, sem = ph.sb, ph.sem
        att_b = sb("att", [P, 2, f])
        prod = sb("prod", [P, f])
        wa = sb("wa", [P, kc, na])
        rows = [sb(f"rows{u}", [P, kc * P]) for u in range(2)]
        turned = [sb(f"turned{u}", [P, kc, P]) for u in range(2)]
        stage = [sb(f"stage{u}", [P, f]) for u in range(2)] if features else None
        lstage = [sb(f"lstage{u}", [P, na + heads]) for u in range(2)]
        tp = [ph.ps(f"tp{u}", [P, kc, P]) for u in range(2)]
        lp = [ph.ps(f"lp{u}", [P, 512]) for u in range(2)]
        fp = [ph.ps(f"fp{u}", [P, 512]) for u in range(2)] if features else None
        wsem, step, folded = sem("weights"), sem("step"), sem("folded")
        rows_turned, turned_ready = sem("rows_turned"), sem("turned_ready")
        logits_done, feats_done, logits_free, feats_free = sem("logits_done"), sem("feats_done"), sem("logits_free"), sem("feats_free")
        staged_l = sem("staged_l")
        stored = [sem(f"stored{u}") for u in range(2)]
        stage_free = sem("stage_free")
        ex = extra(ph)
        block = ph.block()
        nload = len(wload(w)) + len(attload(att_b)) + len(ex.loads)
        stores = (1 if tabs is not None else 0) + 1 + (1 if features else 0)
        post = (3 if selfloop else 1) + (1 if keep else 0) + (0 if tabs is not None else 1)

        @block.sync
        def _(sp):
            with nc.allow_non_contiguous_dma(reason="weights"):
                for out, src in wload(w) + attload(att_b) + ex.loads:
                    sp.dma_start(out, src).then_inc(wsem, 16)
            with sp.Fori(0, T // 2) as i:
                for u in range(2):
                    t = i * 2 + u
                    sp.wait_ge(staged_l, t + 1)
                    if tabs is not None:
                        sp.dma_start(tabs[ds(t * P, P), :], lstage[u][:, 0:heads]).then_inc(stored[u], 16)
                    sp.dma_start(tabd[ds(t * P, P), :], lstage[u][:, heads:heads + tabd.shape[1]]).then_inc(stored[u], 16)
                    if features:
                        sp.wait_ge(feats_free, t + 3)
                        sp.dma_start(table[ds(t * P, P), :], stage[u][:, :]).then_inc(stored[u], 16)
                for u in range(2):
                    sp.wait_ge(stored[u], (i + 1) * (16 * stores))
                    sp.sem_inc(stage_free, 1)

        @block.gpsimd
        def _(pool):
            with pool.Fori(0, T // 2) as i:
                for u in range(2):
                    ex.load(pool, i, u)

        @block.vector
        def _(dve):
            link = Steps(dve, step)
            dve.wait_ge(wsem, 16 * nload)
            for k in range(kc):
                for s in range(2):
                    link(nc.vector.tensor_tensor(prod[:, :], w[:, k, :], att_b[:, s, :], ALU.mult))
                    link(nc.vector.tensor_reduce(wa[:, k, s * heads:(s + 1) * heads],
                                                 prod[:, :].rearrange("p (h d) -> p h d", d=hw), AX_X, ALU.add))
            dve.sem_inc(folded, 1)
            dve.sem_inc(logits_free, 2)
            if hasattr(ex, "own_free"):
                dve.sem_inc(ex.own_free, 2)
            base = link.n
            per = 2 * (ex.steps + post)
            with dve.Fori(0, T // 2) as i:
                link = Steps(dve, step, i * per + base)
                prep(dve, ex, link, i, rows)
                assert link.n == 2 * ex.steps, link.n
                for u in range(2):
                    t = i * 2 + u
                    dve.wait_ge(rows_turned, t + 1)
                    nc.vector.tensor_copy(turned[u][:, :, :], tp[u][:, :, :]).then_inc(turned_ready, 1)
                for u in range(2):
                    t = i * 2 + u
                    if keep:
                        dve.wait_ge(turned_ready, t + 1)
                        link(nc.vector.tensor_copy(xt[:, :, ds(t * P, P)], turned[u][:, :, :]))
                    dve.wait_ge(logits_done, t + 1)
                    dve.wait_ge(stage_free, t + 1)
                    link(nc.vector.tensor_copy(lstage[u][:, 0:na], lp[u][:, 0:na]))
                    if selfloop:
                        a, b, c = (lstage[u][:, s * heads:(s + 1) * heads] for s in range(3))
                        link(nc.vector.tensor_tensor(c, a, b, ALU.add))
                        link(nc.vector.scalar_tensor_tensor(out=c, in0=c, scalar=SLOPE, in1=c, op0=ALU.mult, op1=ALU.max))
                    if tabs is None:
                        link(nc.vector.tensor_copy(g.look[:, ds(t, 1), 0:heads].rearrange("p a h -> p (a h)"), lstage[u][:, 0:heads]))
                    dve.sem_inc(staged_l, 1)
                    dve.sem_inc(logits_free, 1)

        @block.scalar
        def _(act):
            act.sem_inc(feats_free, 2)
            act.sem_inc(stage_free, 2)
            if features or hasattr(ex, "own_free"):
                with act.Fori(0, T // 2) as i:
                    ex.activate(act, i)
                    for u in range(2):
                        if features:
                            t = i * 2 + u
                            act.wait_ge(stage_free, t + 1)
                            act.wait_ge(feats_done, t + 1)
                            nc.scalar.copy(stage[u][:, :], fp[u][:, 0:f]).then_inc(feats_free, 1)

        @block.tensor
        def _(pe):
            pe.wait_ge(folded, 1)
            with pe.Fori(0, T // 2) as i:
                for u in range(2):
                    pe.wait_ge(ex.rows_ready, i * 2 + (u + 1))
                    for k in range(kc):
                        ins = nc.tensor.transpose(tp[u][:, k, :], rows[u][:, k * P:(k + 1) * P], g.ident[:, :])
                    ins.then_inc(rows_turned, 1)
                for u in range(2):
                    t = i * 2 + u
                    pe.wait_ge(turned_ready, t + 1)
                    pe.wait_ge(logits_free, t + 1)
                    for k in range(kc):
                        ins = nc.tensor.matmul(lp[u][:, 0:na], turned[u][:, k, :], wa[:, k, :], start=(k == 0), stop=(k == kc - 1))
                    ins.then_inc(logits_done, 1)
                if features:
                    for u in range(2):
                        pe.wait_ge(feats_free, i * 2 + (u + 1))
                        for k in range(kc):
                            ins = nc.tensor.matmul(fp[u][:, 0:f], turned[u][:, k, :], w[:, k, :], start=(k == 0), stop=(k == kc - 1))
                        ins.then_inc(feats_done, 1)


def edge_alphas(nc, g, name, heads, dwidth, selfloop, typed, tabs, tabd, spread, src_low, feats, alpha):
    with Phase(nc, name + "_logits") as ph:
        sb, sem = ph.sb, ph.sem
        eb = sb("eb", [P, C, heads])
        ea = sb("ea", [ROWS, heads, COLS])
        ed = sb("ed", [ROWS, heads, COLS])
        esa = sb("esa", [ROWS, heads, COLS]) if selfloop else None
        tmp = sb("tmp", [ROWS, heads, COLS]) if typed else None
        dpart = min(dwidth, 16)
        scratch = sb("scratch", [ROWS, max(2 * heads, dpart) * COLS])
        fw = scratch[:, 0:heads * COLS].rearrange("r (h c) -> r h c", c=COLS)
        bw = scratch[:, heads * COLS:2 * heads * COLS].rearrange("r (h c) -> r h c", c=COLS)
        spr = scratch[:, 0:dpart * COLS].rearrange("r (c w) -> r c w", w=dpart)
        mask = sb("mask", [ROWS, COLS]) if typed else None
        node_rows = sb("node_rows", [P, T, dwidth])
        init = sb("init", [ROWS, dwidth])
        ends = sb("ends", [ROWS, 2, heads])
        carry = sb("carry", [ROWS, 2, heads])
        rowst = sb("rowst", [heads, 2, ROWS + 1])
        tps = [ph.ps(f"tps{j}", [P, 512]) for j in range(2)]
        ends_ps = ph.ps("ends_ps", [P, 4, P])
        carry_ps = ends_ps[0:ROWS, 2, 0:2 * heads].rearrange("p (s h) -> p s h", s=2)
        landed = ph.gathers(g, 2)
        scattered, inited = ph.gathers(g, 2, "placed")
        step, spread_loaded, rows_loaded = sem("step"), sem("spread_loaded"), sem("rows_loaded")
        turned, untangled = sem("turned"), sem("untangled")
        ends_ready, ends_turned, rows_done, carry_turned = sem("ends_ready"), sem("ends_turned"), sem("rows_done"), sem("carry_turned")
        expin, expd, alpha_ready, aturned = sem("expin"), sem("expd"), sem("alpha_ready"), sem("aturned")
        sources_done, spread_free = sem("sources_done"), sem("spread_free")
        src = (Gathered if typed else LookedUp)(nc, g, ph, heads, tabs, src_low, eb, landed, sources_done)
        fz = feats(ph) if feats else None
        block = ph.block()

        @block.sync
        def _(sp):
            sp.dma_start(node_rows[:, :, :], tabd.rearrange("(t p) w -> p t w", p=P)).then_inc(rows_loaded, 16)
            sp.wait_ge(scattered, 16 * T)
            for part in range(dwidth // dpart):
                sp.wait_ge(spread_free, part + 1)
                with nc.allow_non_contiguous_dma(reason="some columns of the rows"):
                    sp.dma_start(spr[:, :, :], spread[0:ROWS * COLS, part * dpart:(part + 1) * dpart].rearrange("(r c) w -> r c w", c=COLS)
                                 ).then_inc(spread_loaded, 16)
            src.sync(sp)
            if fz:
                fz.sync(sp)

        @block.gpsimd
        def _(pool):
            pool.wait_ge(rows_loaded, 16)
            for t in range(T):
                nc.gpsimd.indirect_dma_start(out=spread, out_offset=bass.IndirectOffsetOnAxis(ap=g.first[:, t:t + 1], axis=0),
                                             in_=node_rows[:, t, :], in_offset=None).then_inc(scattered, 16)
            nc.gpsimd.indirect_dma_start(out=init[:, :], out_offset=None, in_=tabd,
                                         in_offset=bass.IndirectOffsetOnAxis(ap=g.before[:, :], axis=0)).then_inc(inited, 16)
            src.gpsimd(pool)

        @block.tensor
        def _(pe):
            if fz:
                fz.tensor(pe)
            src.tensor(pe)
            pe.wait_ge(sources_done, 1)
            for h in range(heads):
                if h >= 2:
                    pe.wait_ge(untangled, h - 1)
                v = eb[:, :, h].rearrange("q (r k) -> q k r", k=KB)
                for k in range(KB):
                    ins = nc.tensor.transpose(tps[h % 2][0:ROWS, k * P:(k + 1) * P], v[:, k, :], g.ident[:, :])
                ins.then_inc(turned, 1)
            for r in range(2):
                pe.wait_ge(ends_ready, r + 1)
                for s in range(2):
                    ins = nc.tensor.transpose(ends_ps[0:heads, s, 0:ROWS], ends[:, s, :], g.ident[0:ROWS, 0:ROWS])
                ins.then_inc(ends_turned, 1)
                pe.wait_ge(rows_done, r + 1)
                nc.tensor.transpose(carry_ps[:, 0, :], rowst[:, 0, 0:ROWS], g.ident[0:heads, 0:heads])
                nc.tensor.transpose(carry_ps[:, 1, :], rowst[:, 1, 1:ROWS + 1], g.ident[0:heads, 0:heads]).then_inc(carry_turned, 1)
            for h in range(heads):
                pe.wait_ge(alpha_ready, h + 1)
                pe.wait_ge(untangled, heads if h < 2 else heads + h - 1)
                for k in range(KB):
                    ins = nc.tensor.transpose(tps[h % 2][:, k * P:k * P + ROWS], ea[:, h, k * P:(k + 1) * P], g.ident[0:ROWS, 0:ROWS])
                ins.then_inc(aturned, 1)

        @block.scalar
        def _(act):
            src.scalar(act)
            act.wait_ge(expin, 1)
            nc.scalar.activation(ea[:, :, :], ea[:, :, :], ACT.Exp).then_inc(expd, 1)
            if selfloop:
                nc.scalar.activation(esa[:, :, :], esa[:, :, :], ACT.Exp).then_inc(expd, 1)

        @block.vector
        def _(dve):
            link = Steps(dve, step)
            dve.sem_inc(spread_free, 1)
            if typed:
                link(nc.vector.memset(eb[:, CU:C, :], 0.0))
            dve.wait_ge(inited, 16)
            for r in range(R if typed else 1):
                if r * heads % dpart == 0:
                    dve.wait_ge(spread_loaded, 16 * (r * heads // dpart + 1))
                outs = [(tmp if typed else ed)[:, h, :] for h in range(heads)] + ([esa[:, h, :] for h in range(heads)] if selfloop else [])
                for a, out in enumerate(outs):
                    col = r * heads + a
                    nc.vector.tensor_tensor_scan(out, g.same[:, 0:COLS], spr[:, :, col % dpart], init[:, col:col + 1],
                                                 ALU.mult, ALU.add).then_inc(step, 1)
                    link.n += 1
                dve.wait_ge(step, link.n)
                if (r + 1) * heads % dpart == 0:
                    dve.sem_inc(spread_free, 1)
                if typed:
                    link(nc.vector.tensor_scalar(mask[:, :], g.typr[:, :], float(r), None, ALU.is_equal))
                    own = mask[:, :].rearrange("r (a c) -> r a c", a=1).to_broadcast([ROWS, heads, COLS])
                    if r:
                        link(nc.vector.tensor_tensor(tmp[:, :, :], tmp[:, :, :], own, ALU.mult))
                        link(nc.vector.tensor_tensor(ed[:, :, :], ed[:, :, :], tmp[:, :, :], ALU.add))
                    else:
                        link(nc.vector.tensor_tensor(ed[:, :, :], tmp[:, :, :], own, ALU.mult))
            if fz:
                fz.vector(dve)
            src.vector(dve)
            for h in range(heads):
                dve.wait_ge(turned, h + 1)
                nc.vector.tensor_tensor(ea[:, h, :], ed[:, h, :], tps[h % 2][0:ROWS, :], ALU.add).then_inc(untangled, 1)
            dve.wait_ge(untangled, heads)
            link(nc.vector.scalar_tensor_tensor(out=ea[:, :, :], in0=ea[:, :, :], scalar=SLOPE, in1=ea[:, :, :],
                                                op0=ALU.mult, op1=ALU.max))

            def scans(gaps, rowgaps, op0, op1, start, rnd):
                ahead, back = gaps[:, 0:COLS], gaps[:, COLS:0:-1]

                def both(init):
                    for h in range(heads):
                        nc.vector.tensor_tensor_scan(fw[:, h, :], ahead, ea[:, h, :], init(0, h), op0, op1).then_inc(step, 1)
                        nc.vector.tensor_tensor_scan(bw[:, h, ::-1], back, ea[:, h, ::-1], init(1, h), op0, op1).then_inc(step, 1)
                        link.n += 2
                    dve.wait_ge(step, link.base + link.n)

                both(lambda s, h: start)
                link(nc.vector.tensor_copy(ends[:, 0, :], fw[:, :, COLS - 1]))
                link(nc.vector.tensor_copy(ends[:, 1, :], bw[:, :, 0]))
                dve.sem_inc(ends_ready, 1)
                link(nc.vector.memset(rowst[:, :, :], start))
                dve.wait_ge(ends_turned, rnd + 1)
                link(nc.vector.tensor_tensor_scan(rowst[:, 0, 1:ROWS + 1], rowgaps[0:heads, 0, :], ends_ps[0:heads, 0, 0:ROWS], start, op0, op1))
                link(nc.vector.tensor_tensor_scan(rowst[:, 1, ROWS - 1::-1], rowgaps[0:heads, 1, ::-1],
                                                  ends_ps[0:heads, 1, ROWS - 1::-1], start, op0, op1))
                dve.sem_inc(rows_done, 1)
                dve.wait_ge(carry_turned, rnd + 1)
                link(nc.vector.tensor_copy(carry[:, :, :], carry_ps))
                both(lambda s, h: carry[:, s, h:h + 1])

            scans(g.apart, g.rowapart, ALU.add, ALU.max, -FAR, 0)
            link(nc.vector.tensor_tensor(fw[:, :, :], fw[:, :, :], bw[:, :, :], ALU.max))
            if selfloop:
                link(nc.vector.tensor_tensor(fw[:, :, :], fw[:, :, :], esa[:, :, :], ALU.max))
                link(nc.vector.tensor_tensor(esa[:, :, :], esa[:, :, :], fw[:, :, :], ALU.subtract))
            link(nc.vector.tensor_tensor(ea[:, :, :], ea[:, :, :], fw[:, :, :], ALU.subtract))
            dve.sem_inc(expin, 1)
            dve.wait_ge(expd, 2 if selfloop else 1)
            scans(g.same, g.rowsame, ALU.mult, ALU.add, 0.0, 1)
            link(nc.vector.tensor_tensor(fw[:, :, :], fw[:, :, :], bw[:, :, :], ALU.add))
            link(nc.vector.tensor_tensor(fw[:, :, :], fw[:, :, :], ea[:, :, :], ALU.subtract))
            if selfloop:
                link(nc.vector.tensor_tensor(fw[:, :, :], fw[:, :, :], esa[:, :, :], ALU.add))
            link(nc.vector.reciprocal(bw[:, :, :], fw[:, :, :]))
            for h in range(heads):
                nc.vector.tensor_tensor(ea[:, h, :], ea[:, h, :], bw[:, h, :], ALU.mult).then_inc(alpha_ready, 1)
            for h in range(heads):
                dve.wait_ge(aturned, h + 1)
                nc.vector.tensor_copy(alpha[:, :, h].rearrange("q (r k) -> q k r", k=KB),
                                      tps[h % 2][:, :].rearrange("q (k r) -> q k r", k=KB)[:, :, 0:ROWS]).then_inc(untangled, 1)
            dve.wait_ge(untangled, 2 * heads)


class Gathered:

    def __init__(self, nc, g, ph, heads, tabs, src_low, eb, landed, done):
        self.nc, self.g, self.tabs, self.eb, self.landed, self.done = nc, g, tabs, eb, landed, done
        self.ring = [ph.sb(f"gring{u}", [P, BATCH, heads]) for u in range(2)]
        self.cur = [ph.sb(f"gcur{u}", [P, BATCH], I32) for u in range(2)]
        self.ring_free, self.copied, self.issued, self.taken = (
            ph.sem(s) for s in ("ring_free", "copied", "issued", "taken"))

    def sync(self, sp):
        pass

    def tensor(self, pe):
        pass

    def vector(self, dve):
        pass

    def gpsimd(self, pool):
        with pool.Fori(0, CU // (2 * BATCH)) as i:
            for u in range(2):
                n = i * 2 + u
                pool.wait_ge(self.copied, n + 1)
                pool.sem_inc(self.issued, 1)
                for b in range(BATCH):
                    self.nc.gpsimd.indirect_dma_start(out=self.ring[u][:, b, :], out_offset=None, in_=self.tabs,
                                                      in_offset=bass.IndirectOffsetOnAxis(ap=self.cur[u][:, b:b + 1], axis=0)
                                                      ).then_inc(self.landed[u], 16)

    def scalar(self, act):
        nc = self.nc
        for u in range(2):
            nc.scalar.copy(self.cur[u][:, :], self.g.srct[:, u * BATCH:(u + 1) * BATCH]).then_inc(self.copied, 1)

        def take(n, i, u, last):
            act.wait_ge(self.landed[u], (i + 1) * (16 * BATCH))
            act.sem_inc(self.taken, 1)
            nc.scalar.copy(self.eb[:, ds(n * BATCH, BATCH), :], self.ring[u][:, :, :]).then_inc(self.ring_free, 1)
            if not last:
                act.wait_ge(self.ring_free, n + 1)
                act.sem_inc(self.taken, 1)
                nc.scalar.copy(self.cur[u][:, :], self.g.srct[:, ds((n + 2) * BATCH, BATCH)]).then_inc(self.copied, 1)

        turns = CU // (2 * BATCH)
        with act.Fori(0, turns - 1) as i:
            for u in range(2):
                take(i * 2 + u, i, u, False)
        for u in range(2):
            take((turns - 1) * 2 + u, turns - 1, u, True)
        act.wait_ge(self.ring_free, turns * 2)
        act.sem_inc(self.done, 1)


BLK = 8
BLOCKS = C // BLK
assert C % BLK == 0 and BLOCKS % 2 == 1


class LookedUp:

    def __init__(self, nc, g, ph, heads, tabs, src_low, eb, landed, done):
        self.nc, self.g, self.src_low, self.eb, self.done, self.heads = nc, g, src_low, eb, done, heads
        sb, sem = ph.sb, ph.sem
        self.lc = min(BLK, 512 // (HIGH * heads))
        self.steps = BLK // self.lc
        self.low = [sb(f"low{u}", [P, BLK * P], BF16) for u in range(2)]
        self.onehot = [[sb(f"onehot{u}_{k}", [P, BLK, P], BF16) for k in range(2)] for u in range(2)]
        self.parts = [sb(f"part{s}", [P, T, heads], BF16) for s in range(3)]
        self.left = sb("left", [P, T, heads])
        self.places = sb("places", [P, 2])
        self.bits, self.high = sb("bits", [P, C], I32), sb("high", [P, C])
        self.pick = sb("pick", [P, self.lc, HIGH])
        self.chosen = sb("chosen", [P, self.lc, HIGH, heads])
        self.ps = [ph.ps(f"lps{u}", [P, 512]) for u in range(2)]
        self.step, self.made, self.ready, self.looked, self.free, self.chose = (
            sem(s) for s in ("lstep", "lmade", "lready", "looked", "lfree", "chose"))
        self.loaded = [sem(f"lloaded{u}") for u in range(2)]

    def gpsimd(self, pool):
        pass

    def scalar(self, act):
        pass

    def sync(self, sp):
        def load(n, u):
            sp.wait_ge(self.made, n + 1)
            sp.dma_start(self.low[u][:, :], row_of(self.src_low)[:, ds(n * (BLK * P), BLK * P)]).then_inc(self.loaded[u], 16)

        with sp.Fori(0, BLOCKS // 2) as i:
            for u in range(2):
                load(i * 2 + u, u)
        load(BLOCKS - 1, 0)

    def tensor(self, pe):
        def block(n, u):
            pe.wait_ge(self.made, n + 3)
            for s in range(self.steps):
                m = n * self.steps + s
                pe.wait_ge(self.free, m + 1)
                for b in range(self.lc):
                    out = self.ps[self.bank(u, s)][:, b * HIGH * self.heads:(b + 1) * HIGH * self.heads]
                    for k in range(2):
                        for part in range(3):
                            rhs = self.parts[part][:, :, :].rearrange("p (t k) h -> p k t h", k=2)[:, k, :, :]
                            ins = self.nc.tensor.matmul(out, self.onehot[u][k][:, s * self.lc + b, :], rhs,
                                                        start=(k == 0 and part == 0), stop=(k == 1 and part == 2))
                ins.then_inc(self.looked, 1)

        pe.wait_ge(self.ready, 1)
        with pe.Fori(0, BLOCKS // 2) as i:
            for u in range(2):
                block(i * 2 + u, u)
        block(BLOCKS - 1, 0)

    def bank(self, u, s):
        return (u * self.steps + s) % 2

    def vector(self, dve):
        nc, g, heads = self.nc, self.g, self.heads
        link = Steps(dve, self.step)
        link(nc.vector.tensor_copy(self.parts[0][:, :, :], g.look[:, :, 0:heads]))
        link(nc.vector.tensor_tensor(self.left[:, :, :], g.look[:, :, 0:heads], self.parts[0][:, :, :], ALU.subtract))
        link(nc.vector.tensor_copy(self.parts[1][:, :, :], self.left[:, :, :]))
        link(nc.vector.tensor_tensor(self.left[:, :, :], self.left[:, :, :], self.parts[1][:, :, :], ALU.subtract))
        link(nc.vector.tensor_copy(self.parts[2][:, :, :], self.left[:, :, :]))
        link(nc.vector.tensor_copy(self.places[:, 0:1], g.pcol[:, :]))
        link(nc.vector.tensor_scalar(self.places[:, 1:2], g.pcol[:, :], float(P), None, ALU.add))
        link(nc.vector.tensor_scalar(self.bits[:, :], g.srci[:, :], LOW.bit_length() - 1, None, ALU.arith_shift_right))
        link(nc.vector.tensor_copy(self.high[:, :], self.bits[:, :]))
        dve.sem_inc(self.ready, 1)
        dve.sem_inc(self.made, 2)
        dve.sem_inc(self.looked, 2 * self.steps)
        dve.sem_inc(self.free, 2)
        base = link.n

        def make(n, i, u):
            dve.wait_ge(self.loaded[u], (i + 1) * 16)
            dve.wait_ge(self.looked, (n + 1) * self.steps)
            dve.sem_inc(self.chose, 1)
            for k in range(2):
                ins = nc.vector.tensor_scalar(self.onehot[u][k][:, :, :].rearrange("p b e -> p (b e)"), self.low[u][:, :],
                                              self.places[:, k:k + 1], None, ALU.is_equal)
            ins.then_inc(self.made, 1)

        def choose(n, u):
            for s in range(self.steps):
                m = n * self.steps + s
                link = Steps(dve, self.step, m * 3 + base)
                at = ds(m * self.lc, self.lc)
                link(nc.vector.tensor_tensor(self.pick[:, :, :],
                                             g.nodes[:, 0:HIGH].rearrange("p (b t) -> p b t", b=1).to_broadcast([P, self.lc, HIGH]),
                                             self.high[:, at].rearrange("p (b t) -> p b t", t=1).to_broadcast([P, self.lc, HIGH]),
                                             ALU.is_equal))
                dve.wait_ge(self.looked, m + (2 * self.steps + 1))
                nc.vector.tensor_tensor(self.chosen[:, :, :, :].rearrange("p b t h -> p (b t) h"),
                                        self.ps[self.bank(u, s)][:, 0:self.lc * HIGH * heads].rearrange("p (a h) -> p a h", h=heads),
                                        self.pick[:, :, :].rearrange("p b t -> p (b t)").rearrange("p (a h) -> p a h", h=1)
                                        .to_broadcast([P, self.lc * HIGH, heads]), ALU.mult).then_inc(self.free, 1)
                dve.wait_ge(self.free, m + 3)
                dve.sem_inc(self.step, 1)
                link.n += 1
                link(nc.vector.tensor_reduce(self.eb[:, at, :], self.chosen[:, :, :, :].rearrange("p b t h -> p b h t"), AX_X, ALU.add))

        make(0, 0, 0)
        with dve.Fori(0, BLOCKS // 2) as i:
            make(i * 2 + 1, i, 1)
            choose(i * 2, 0)
            make(i * 2 + 2, i + 1, 0)
            choose(i * 2 + 1, 1)
        choose(BLOCKS - 1, 0)
        dve.sem_inc(self.done, 1)


class Features:

    def __init__(self, nc, g, ph, xt, w, table):
        self.nc, self.g, self.xt, self.w, self.table = nc, g, xt, w, table
        self.kc, self.f = w.shape[1], w.shape[2]
        self.nb = self.f // 512
        self.lhs = [ph.sb(f"lhs{u}", [P, self.kc, P]) for u in range(2)]
        self.stage = [ph.sb(f"fstage{u}", [P, self.f]) for u in range(2)]
        self.fp = [ph.ps(f"fp{b}", [P, 512]) for b in range(self.nb)]
        self.lhs_ready, self.done, self.staged, self.stage_free = (ph.sem(s) for s in ("lhs_ready", "feats_done", "fstaged", "fstage_free"))
        self.stored = [ph.sem(f"fstored{u}") for u in range(2)]

    def sync(self, sp):
        with sp.Fori(0, T // 2) as i:
            for u in range(2):
                t = i * 2 + u
                sp.wait_ge(self.staged, (t + 2) * self.nb)
                sp.dma_start(self.table[ds(t * P, P), :], self.stage[u][:, :]).then_inc(self.stored[u], 16)
            for u in range(2):
                sp.wait_ge(self.stored[u], (i + 1) * 16)
                sp.sem_inc(self.stage_free, 1)

    def tensor(self, pe):
        with pe.Fori(0, T // 2) as i:
            for u in range(2):
                t = i * 2 + u
                pe.wait_ge(self.lhs_ready, t + 1)
                for b in range(self.nb):
                    pe.wait_ge(self.staged, t * self.nb + (b + 1))
                    for k in range(self.kc):
                        ins = self.nc.tensor.matmul(self.fp[b][:, :], self.lhs[u][:, k, :], self.w[:, k, b * 512:(b + 1) * 512],
                                                    start=(k == 0), stop=(k == self.kc - 1))
                    ins.then_inc(self.done, 1)

    def vector(self, dve):
        nc = self.nc
        dve.sem_inc(self.staged, self.nb)
        dve.sem_inc(self.stage_free, 2)

        def lhs(t, u):
            nc.vector.tensor_copy(self.lhs[u][:, :, :], self.xt[:, :, ds(t * P, P)]).then_inc(self.lhs_ready, 1)

        def stage(t, u):
            dve.wait_ge(self.stage_free, t + 1)
            for b in range(self.nb):
                dve.wait_ge(self.done, t * self.nb + (b + 1))
                nc.vector.tensor_copy(self.stage[u][:, b * 512:(b + 1) * 512], self.fp[b][:, :]).then_inc(self.staged, 1)

        lhs(0, 0)
        lhs(1, 1)
        with dve.Fori(0, T // 2 - 1) as i:
            for u in range(2):
                t = i * 2 + u
                stage(t, u)
                lhs(t + 2, u)
        for u in range(2):
            stage(T - 2 + u, u)


def edge_messages(nc, g, name, heads, f, selfloop, idx, table, alpha, acc):
    na = heads if selfloop else 0
    hw = f // heads
    with Phase(nc, name + "_messages") as ph:
        sb, sem = ph.sb, ph.sem
        ring = [sb(f"ring{u}", [P, G, f]) for u in range(RING)]
        cur = [sb(f"cur{u}", [P, G], I32) for u in range(RING)]
        onehot = [sb(f"onehot{u}", [P, G, P]) for u in range(BUFS)]
        msg = [sb(f"msg{u}", [P, G, f]) for u in range(BUFS)]
        mp = [ph.ps(f"mp{u}", [P, 1024 if na + f > 512 else 512]) for u in range(BUFS)]
        landed = ph.gathers(g, RING)
        indexed, issued, placed = sem("indexed"), sem("issued"), sem("placed")
        cleared, onehot_made, weighted, summed, added = (sem(s) for s in ("cleared", "onehot_made", "weighted", "summed", "added"))
        block = ph.block()

        def steps(engine, i, lag=0):
            regs = [engine.alloc_register(f"{name}_walk{r}") for r in range(2 * (U + lag))]
            engine.load(regs, g.walk[0:1, ds(i * U + (LAG - lag), U + lag), :].rearrange("p s a -> p (s a)"))
            return [(engine.snap(regs[2 * u], min_val=0, max_val=CG - 1), engine.snap(regs[2 * u + 1], min_val=0, max_val=T - 1))
                    for u in range(U + lag)]

        @block.scalar
        def _(act):
            with act.Fori(0, STEPS // U) as i:
                walk = steps(act, i)
                for u in range(U):
                    n, (c, _) = i * U + u, walk[u]
                    act.wait_ge(weighted, n + 1)
                    act.sem_inc(placed, 1)
                    nc.scalar.copy(cur[u % RING][:, :], idx[:, ds(c * G, G)]).then_inc(indexed, 1)

        @block.gpsimd
        def _(pool):
            with pool.Fori(0, STEPS // U) as i:
                for u in range(U):
                    n = i * U + u
                    pool.wait_ge(indexed, n + 1)
                    pool.sem_inc(issued, 1)
                    for b in range(G):
                        nc.gpsimd.indirect_dma_start(out=ring[u % RING][:, b, :], out_offset=None, in_=table,
                                                     in_offset=bass.IndirectOffsetOnAxis(ap=cur[u % RING][:, b:b + 1], axis=0)
                                                     ).then_inc(landed[u % RING], 16)

        @block.vector
        def _(dve):
            nc.vector.memset(acc[:, :, :], 0.0).then_inc(cleared, 1)
            for u in range(BUFS):
                nc.vector.memset(mp[u][:, 0:f + na], 0.0).then_inc(cleared, 1)
            dve.wait_ge(cleared, 1 + BUFS)
            dve.sem_inc(weighted, RING)
            dve.sem_inc(summed, BUFS)
            dve.sem_inc(added, 1)

            def make(n, u, i, c, t):
                dve.wait_ge(summed, n + 1)
                nc.vector.tensor_tensor(onehot[u % BUFS][:, :, :],
                                        g.nodes[:, ds(t * P, P)].rearrange("p (b n) -> p b n", b=1).to_broadcast([P, G, P]),
                                        g.dstb[:, ds(c * G, G)].rearrange("p (b n) -> p b n", n=1).to_broadcast([P, G, P]),
                                        ALU.is_equal).then_inc(onehot_made, 1)
                dve.wait_ge(landed[u % RING], i * (U // RING * 16 * G) + (u // RING + 1) * 16 * G)
                nc.vector.tensor_tensor(msg[u % BUFS][:, :, :].rearrange("p b (h d) -> p (b h) d", d=hw),
                                        ring[u % RING][:, :, :].rearrange("p b (h d) -> p (b h) d", d=hw),
                                        alpha[:, ds(c * G, G), :].rearrange("p b h -> p (b h)")
                                        .rearrange("p (a d) -> p a d", d=1).to_broadcast([P, G * heads, hw]),
                                        ALU.mult).then_inc(weighted, 1)

            def add(n, u, t):
                dve.wait_ge(summed, n + (1 + BUFS - LAG))
                dve.wait_ge(added, n + 1)
                row = acc[:, ds(t, 1), :].rearrange("p a f -> p (a f)")
                nc.vector.tensor_tensor(row, row, mp[(u - LAG) % BUFS][:, 0:f + na], ALU.add).then_inc(added, 1)

            with dve.Fori(0, STEPS // U) as i:
                walk = steps(dve, i, LAG)
                for u in range(U):
                    n, (c, t) = i * U + u, walk[u + LAG]
                    make(n, u, i, c, t)
                    add(n, u, walk[u][1])
            tail = [dve.alloc_register(f"{name}_tail{r}") for r in range(2 * LAG)]
            dve.load(tail, g.walk[0:1, STEPS:STEPS + LAG, :].rearrange("p s a -> p (s a)"))
            for u in range(LAG):
                add(STEPS + u, u, dve.snap(tail[2 * u + 1], min_val=0, max_val=T - 1))
            dve.wait_ge(added, STEPS + LAG + 1)

        @block.tensor
        def _(pe):
            with pe.Fori(0, STEPS // U) as i:
                walk = steps(pe, i) if na else None
                for u in range(U):
                    n, at = i * U + u, u % BUFS
                    pe.wait_ge(onehot_made, n + 1)
                    pe.wait_ge(weighted, n + (RING + 1))
                    pe.wait_ge(added, n + 1 + (LAG - BUFS + 1))
                    for b in range(G):
                        ins = nc.tensor.matmul(mp[at][:, 0:f], onehot[at][:, b, :], msg[at][:, b, :],
                                               start=(b == 0), stop=(b == G - 1))
                    if na:
                        c = walk[u][0]
                        for b in range(G):
                            ins = nc.tensor.matmul(mp[at][:, f:f + na], onehot[at][:, b, :],
                                                   alpha[:, ds(c * G + b, 1), :].rearrange("p a h -> p (a h)"),
                                                   start=(b == 0), stop=(b == G - 1))
                    ins.then_inc(summed, 1)


class PlainTile:

    def __init__(self, ph, steps, consts=()):
        self.steps = steps
        self.rows_ready = ph.sem("rows_ready")
        self.tiles = [ph.sb(f"const{n}", [P, c.shape[0]]) for n, c in enumerate(consts)]
        self.loads = [(t[:, :], row_of(c)) for t, c in zip(self.tiles, consts)]

    def load(self, pool, i, u):
        pass

    def activate(self, act, i):
        pass


class LoadedTile(PlainTile):

    def __init__(self, ph, g, steps, consts, table):
        super().__init__(ph, steps, consts)
        width = table.shape[1]
        self.table = table
        self.own = [ph.sb(f"own{u}", [P, width]) for u in range(2)]
        self.aself = ph.sb("aself", [P, 8])
        self.neg = [ph.sb(f"neg{u}", [P, width]) for u in range(2)]
        self.landed = ph.gathers(g, 2)
        self.neg_ready, self.exp_done, self.own_free = ph.sem("neg_ready"), ph.sem("exp_done"), ph.sem("own_free")

    def load(self, pool, i, u):
        t = i * 2 + u
        pool.wait_ge(self.own_free, t + 1)
        pool.dma_start(self.own[u][:, :], self.table[ds(t * P, P), :]).then_inc(self.landed[u], 16)

    def activate(self, act, i):
        for u in range(2):
            act.wait_ge(self.neg_ready, i * 2 + (u + 1))
            act.activation(self.neg[u][:, :], self.neg[u][:, :], ACT.Exp).then_inc(self.exp_done, 1)


def add_self_loop(nc, link, ex, out, own, acc, heads, f):
    hw = f // heads
    link(nc.vector.tensor_scalar(ex.aself[:, 0:heads], acc[:, f:f + heads], -1.0, 1.0, ALU.mult, ALU.add))
    link(nc.vector.tensor_tensor(own.rearrange("p (h d) -> p h d", d=hw), own.rearrange("p (h d) -> p h d", d=hw),
                                 ex.aself[:, 0:heads].rearrange("p (h a) -> p h a", a=1).to_broadcast([P, heads, hw]), ALU.mult))
    link(nc.vector.tensor_tensor(out, own, acc[:, 0:f], ALU.add))


def route(nc, g, name, prep, prep_steps, ex_make, wr, bo, top2, xt, wts):
    with Phase(nc, name + "_route") as ph:
        sb, sem = ph.sb, ph.sem
        wr_s = sb("wr", [P, 2, R])
        bo_s = sb("bo", [R, D])
        rows = sb("rows", [P, D])
        mv = sb("mv", [P, 4])
        lg, top, topf, topi = sb("lg", [P, R]), sb("top", [P, R]), sb("topf", [P, R]), sb("topi", [P, R], U32)
        dx, one, two, wt = sb("dx", [P, R]), sb("one", [P, R]), sb("two", [P, R]), sb("wt", [P, R])
        wtt = sb("wtt", [R, P])
        tcopy = sb("tcopy", [P, 2, P])
        tp, lp, wp, bp = ph.ps("tp", [P, 2, P]), ph.ps("lp", [P, 512]), ph.ps("wp", [R, P]), ph.ps("bp", [P, 512])
        wsem, step, logits_seen = sem("weights"), sem("step"), sem("logits_seen")
        rows_turned, xt_ready, logits_done = sem("rows_turned"), sem("xt_ready"), sem("logits_done")
        dx_ready, dx_exp, wt_ready, wt_turned, wtt_ready, bias_done = (
            sem(s) for s in ("dx_ready", "dx_exp", "wt_ready", "wt_turned", "wtt_ready", "bias_done"))
        ex = ex_make(ph)
        block = ph.block()
        nload = 2 + len(ex.loads)
        tail = (11 if top2 else 6) + 3
        per = prep_steps + 1 + tail

        @block.sync
        def _(sp):
            with nc.allow_non_contiguous_dma(reason="a small matrix of weights"):
                sp.dma_start(wr_s[:, :, :], wr.rearrange("(k p) e -> p k e", p=P)).then_inc(wsem, 16)
            sp.dma_start(bo_s[:, :], bo).then_inc(wsem, 16)
            for out, src in ex.loads:
                sp.dma_start(out, src).then_inc(wsem, 16)

        @block.scalar
        def _(act):
            with act.Fori(0, T) as t:
                act.wait_ge(dx_ready, t + 1)
                nc.scalar.activation(dx[:, :], dx[:, :], ACT.Exp).then_inc(dx_exp, 1)

        @block.tensor
        def _(pe):
            pe.wait_ge(wsem, 16 * nload)
            with pe.Fori(0, T) as t:
                pe.wait_ge(ex.rows_ready, t + 1)
                for k in range(2):
                    ins = nc.tensor.transpose(tp[:, k, :], rows[:, k * P:(k + 1) * P], g.ident[:, :])
                ins.then_inc(rows_turned, 1)
                pe.wait_ge(xt_ready, t + 1)
                for k in range(2):
                    ins = nc.tensor.matmul(lp[:, 0:R], tcopy[:, k, :], wr_s[:, k, :], start=(k == 0), stop=(k == 1))
                ins.then_inc(logits_done, 1)
                pe.wait_ge(wt_ready, t + 1)
                nc.tensor.transpose(wp[:, :], wt[:, :], g.ident[:, :]).then_inc(wt_turned, 1)
                pe.wait_ge(wtt_ready, t + 1)
                nc.tensor.matmul(bp[:, 0:D], wtt[:, :], bo_s[:, :], start=True, stop=True).then_inc(bias_done, 1)

        @block.vector
        def _(dve):
            dve.wait_ge(wsem, 16 * nload)
            with dve.Fori(0, T // 2) as i:
                for u in range(2):
                    t = i * 2 + u
                    link = Steps(dve, step, t * per)
                    prep(dve, ex, link, i, u, rows)
                    assert link.n == prep_steps, link.n
                    dve.sem_inc(ex.rows_ready, 1)
                    dve.wait_ge(rows_turned, t + 1)
                    link(nc.vector.tensor_copy(tcopy[:, :, :], tp[:, :, :]))
                    dve.sem_inc(xt_ready, 1)
                    link(nc.vector.tensor_copy(xt[:, :, ds(t * P, P)], tcopy[:, :, :]))
                    dve.wait_ge(logits_done, t + 1)
                    link(nc.vector.tensor_tensor(lg[:, :], lp[:, 0:R], ex.tiles[-1][:, :], ALU.add))
                    if top2:
                        dve.sem_inc(logits_seen, 1)
                        link(nc.vector.max(top[:, :], lg[:, :]))
                        dve.sem_inc(logits_seen, 1)
                        link(nc.vector.max_index(topi[:, :], top[:, :], lg[:, :]))
                        link(nc.vector.tensor_copy(topf[:, :], topi[:, :]))
                        link(nc.vector.tensor_tensor(dx[:, :], top[:, :], top[:, 0:1].to_broadcast([P, R]), ALU.subtract))
                        dve.sem_inc(dx_ready, 1)
                        dve.wait_ge(dx_exp, t + 1)
                        link(nc.vector.tensor_scalar(mv[:, 0:1], dx[:, 1:2], 1.0, None, ALU.add))
                        link(nc.vector.reciprocal(mv[:, 1:2], mv[:, 0:1]))
                        link(nc.vector.tensor_tensor(mv[:, 2:3], dx[:, 1:2], mv[:, 1:2], ALU.mult))
                        link(nc.vector.tensor_scalar(one[:, :], g.nodes[:, 0:R], topf[:, 0:1], mv[:, 1:2], ALU.is_equal, ALU.mult))
                        link(nc.vector.tensor_scalar(two[:, :], g.nodes[:, 0:R], topf[:, 1:2], mv[:, 2:3], ALU.is_equal, ALU.mult))
                        link(nc.vector.tensor_tensor(wt[:, :], one[:, :], two[:, :], ALU.add))
                    else:
                        link(nc.vector.tensor_reduce(mv[:, 0:1], lg[:, :], AX_X, ALU.max))
                        link(nc.vector.tensor_scalar(dx[:, :], lg[:, :], mv[:, 0:1], None, ALU.subtract))
                        dve.sem_inc(dx_ready, 1)
                        dve.wait_ge(dx_exp, t + 1)
                        link(nc.vector.tensor_reduce(mv[:, 1:2], dx[:, :], AX_X, ALU.add))
                        link(nc.vector.reciprocal(mv[:, 2:3], mv[:, 1:2]))
                        link(nc.vector.tensor_scalar(wt[:, :], dx[:, :], mv[:, 2:3], None, ALU.mult))
                    dve.sem_inc(wt_ready, 1)
                    link(nc.vector.tensor_copy(wts[:, :, ds(t, 1)], wt[:, :].rearrange("p (e a) -> p e a", a=1)))
                    dve.wait_ge(wt_turned, t + 1)
                    nc.vector.tensor_copy(wtt[:, :], wp[:, :]).then_inc(wtt_ready, 1)
                    dve.wait_ge(bias_done, t + 1)
                    xrow = g.x[:, ds(t, 1), :].rearrange("p a f -> p (a f)")
                    link(nc.vector.tensor_tensor(xrow, xrow, bp[:, 0:D], ALU.add))
                    assert link.n == per, (link.n, per)


CT = 3
CN = CT * P
NB = T // CT // 2


def experts(nc, g, name, layers, loads, affine, params, xt, wts):
    with Phase(nc, name + "_experts") as ph:
        sb, sem = ph.sb, ph.sem
        depth = len(layers)
        w = [[sb(f"w{u}_{l}", [P, kc, mc * P]) for l, (kc, mc) in enumerate(layers)] for u in range(2)]
        wo = [sb(f"wo{u}", [P, layers[-1][1], D]) for u in range(2)]
        hid = [[sb(f"hid{a}_{l}", [P, mc, CN]) for l, (kc, mc) in enumerate(layers)] for a in range(2)]
        ncol = sum(mc for _, mc in layers)
        slot = sb("slot", [P, 2, 2, ncol])
        table = sb("table", [P, 2, R, ncol])
        up = [ph.ps(f"up{b}", [P, 512]) for b in range(4)]
        yp = [ph.ps(f"yp{b}", [P, 512]) for b in range(CT)]
        wsem = [sem(f"weights{u}") for u in range(2)]
        expert_free, up_done, act_done, y_done, y_added = (
            sem(s) for s in ("expert_free", "up_done", "act_done", "y_done", "y_added"))
        params_ready, slotted, expert_begun = sem("params_ready"), sem("slotted"), sem("expert_begun")
        pz = params.start(ph, table, params_ready)
        groups = 2 * ncol
        assert groups == 8
        block = ph.block()

        @block.sync
        def _(sp):
            params.sync(sp, pz)
            with sp.Fori(0, R // 2) as i:
                for u in range(2):
                    e = i * 2 + u
                    sp.wait_ge(expert_free, e + 1)
                    for l in range(depth):
                        sp.dma_start(w[u][l][:, :, :], loads[l][ds(e, 1), :, :].rearrange("a (k p) f -> p (a k) f", p=P)).then_inc(wsem[u], 16)
                    sp.dma_start(wo[u][:, :, :], loads[depth][ds(e, 1), :, :].rearrange("a (k p) f -> p (a k) f", p=P)).then_inc(wsem[u], 16)

        @block.tensor
        def _(pe):
            params.tensor(pe, pz)
            pe.sem_inc(expert_free, 2)
            pe.sem_inc(y_done, 2 * CT)
            with pe.Fori(0, R // 2) as i:
                for u in range(2):
                    e = i * 2 + u
                    pe.wait_ge(wsem[u], (i + 1) * (16 * (depth + 1)))
                    pe.sem_inc(expert_begun, 1)
                    with pe.Fori(0, NB) as c:
                        q = e * NB + c
                        n = 0
                        for l, (kc, mc) in enumerate(layers):
                            for a in range(2):
                                if l:
                                    pe.wait_ge(act_done, q * groups + (4 + before + (a + 1) * kc))
                                for m in range(mc):
                                    pe.wait_ge(act_done, q * groups + (n + 1))
                                    for k in range(kc):
                                        rhs = hid[a][l - 1][:, k, :] if l else xt[:, k, ds((c * 2 + a) * CN, CN)]
                                        ins = nc.tensor.matmul(up[n % 4][:, 0:CN], w[u][l][:, k, m * P:(m + 1) * P], rhs,
                                                               start=(k == 0), stop=(k == kc - 1))
                                    ins.then_inc(up_done, 1)
                                    n += 1
                            before = n - 2 * mc
                        mc = layers[-1][1]
                        for a in range(2):
                            pe.wait_ge(act_done, q * groups + (4 + before + (a + 1) * mc))
                            for j in range(CT):
                                pe.wait_ge(y_added, q * (2 * CT) + (a * CT + j + 1))
                                for k in range(mc):
                                    ins = nc.tensor.matmul(yp[j][:, 0:D], hid[a][-1][:, k, j * P:(j + 1) * P], wo[u][:, k, :],
                                                           start=(k == 0), stop=(k == mc - 1))
                                ins.then_inc(y_done, 1)
                    pe.wait_ge(y_done, (e + 1) * (NB * 2 * CT) + 2 * CT)
                    pe.sem_inc(expert_free, 1)

        @block.scalar
        def _(act):
            act.sem_inc(act_done, 4)
            params.scalar(act, pz)
            act.wait_ge(params_ready, params.ready)
            with act.Fori(0, R // 2) as i:
                for u in range(2):
                    e = i * 2 + u
                    nc.scalar.copy(slot[:, u, :, :], table[:, :, ds(e, 1), :].rearrange("p s a c -> p s (a c)")).then_inc(slotted, 1)
                    act.wait_ge(slotted, e + 1)
                    with act.Fori(0, NB) as c:
                        q = e * NB + c
                        n = col = 0
                        for l, (kc, mc) in enumerate(layers):
                            for a in range(2):
                                act.wait_ge(y_done, q * (2 * CT) + (a + 1) * CT)
                                for m in range(mc):
                                    act.wait_ge(up_done, q * groups + (n + 1))
                                    if affine:
                                        nc.scalar.activation(hid[a][l][:, m, :], up[n % 4][:, 0:CN], ACT.Relu,
                                                             bias=slot[:, u, 0, col + m:col + m + 1],
                                                             scale=slot[:, u, 1, col + m:col + m + 1]).then_inc(act_done, 1)
                                    else:
                                        nc.scalar.activation(hid[a][l][:, m, :], up[n % 4][:, 0:CN], ACT.Gelu,
                                                             bias=slot[:, u, 0, col + m:col + m + 1]).then_inc(act_done, 1)
                                    n += 1
                            col += mc

        @block.vector
        def _(dve):
            params.vector(dve, pz)
            dve.sem_inc(y_added, CT)
            with dve.Fori(0, R) as e:
                with dve.Fori(0, NB) as c:
                    for n in range(2 * CT):
                        k = (e * NB + c) * (2 * CT) + n
                        t = c * (2 * CT) + n
                        dve.wait_ge(y_done, k + (2 * CT + 1))
                        dve.wait_ge(y_added, k + CT)
                        xrow = g.x[:, ds(t, 1), :].rearrange("p a f -> p (a f)")
                        nc.vector.scalar_tensor_tensor(out=xrow, in0=yp[n % CT][:, 0:D],
                                                       scalar=wts[:, ds(e, 1), ds(t, 1)].rearrange("p a b -> p (a b)"),
                                                       in1=xrow, op0=ALU.mult, op1=ALU.add).then_inc(y_added, 1)
            dve.wait_ge(y_added, R * NB * 2 * CT + CT)


class GeluParams:

    ready = 1

    def __init__(self, nc, g, b1):
        self.nc, self.g, self.b1 = nc, g, b1

    def start(self, ph, table, ready):
        m = self.b1.shape[1] // P
        self.m, self.table, self.done = m, table, ready
        return {"raw": ph.sb("raw", [R * m, P]), "tp": ph.ps("ptp", [P, 512]),
                "loaded": ph.sem("p_loaded"), "turned": ph.sem("p_turned")}

    def scalar(self, act, z):
        pass

    def sync(self, sp, z):
        sp.dma_start(z["raw"][:, :], self.b1.rearrange("e (m p) -> (e m) p", p=P)).then_inc(z["loaded"], 16)

    def tensor(self, pe, z):
        pe.wait_ge(z["loaded"], 16)
        n = R * self.m
        pe.transpose(z["tp"][:, 0:n], z["raw"][:, :], self.g.ident[0:n, 0:n]).then_inc(z["turned"], 1)

    def vector(self, dve, z):
        dve.wait_ge(z["turned"], 1)
        self.nc.vector.memset(self.table[:, 1, :, :], 1.0).then_inc(z["turned"], 1)
        dve.wait_ge(z["turned"], 2)
        self.nc.vector.tensor_copy(self.table[:, 0, :, :], z["tp"][:, 0:R * self.m].rearrange("p (e m) -> p e m", m=self.m)
                                   ).then_inc(self.done, 1)


class NormParams:

    ready = 4
    EPS = 1e-3

    def __init__(self, nc, g, layers):
        self.nc, self.g, self.layers = nc, g, layers

    def start(self, ph, table, ready):
        self.table, self.done = table, ready
        n = R * 2
        return {"raw": [[ph.sb(f"raw{l}_{s}", [n, P]) for s in range(5)] for l in range(2)],
                "tp": ph.ps("ptp", [P, 4, R * 2]), "loaded": ph.sem("p_loaded"), "turned": ph.sem("p_turned"),
                "step": ph.sem("p_step"), "ready": ph.sem("p_ready"),
                "var_ready": ph.sem("p_var_ready"), "rooted": ph.sem("p_rooted")}

    def scalar(self, act, z):
        for l in range(2):
            act.wait_ge(z["var_ready"], l + 1)
            v = z["raw"][l][4]
            act.activation(v[:, :], v[:, :], ACT.Sqrt).then_inc(z["rooted"], 1)

    def sync(self, sp, z):
        for l in range(2):
            for tile, vec in zip(z["raw"][l], self.layers[l]):
                sp.dma_start(tile[:, :], vec.rearrange("e (m p) -> (e m) p", p=P)).then_inc(z["loaded"], 16)

    def vector(self, dve, z):
        nc, link = self.nc, Steps(dve, z["step"])
        dve.wait_ge(z["loaded"], 160)
        for l in range(2):
            b, gm, be, m, v = (t[:, :] for t in z["raw"][l])
            link(nc.vector.tensor_scalar(v, v, self.EPS, None, ALU.add))
            dve.sem_inc(z["var_ready"], 1)
            dve.wait_ge(z["rooted"], l + 1)
            link(nc.vector.reciprocal(v, v))
            link(nc.vector.tensor_tensor(gm, gm, v, ALU.mult))
            link(nc.vector.tensor_tensor(b, b, m, ALU.subtract))
            link(nc.vector.tensor_tensor(b, b, gm, ALU.mult))
            link(nc.vector.tensor_tensor(b, b, be, ALU.add))
        dve.sem_inc(z["ready"], 1)
        dve.wait_ge(z["turned"], 1)
        for l in range(2):
            for s in range(2):
                nc.vector.tensor_copy(self.table[:, s, :, l * 2:l * 2 + 2],
                                      z["tp"][:, l * 2 + s, :].rearrange("p (e m) -> p e m", m=2)).then_inc(self.done, 1)

    def tensor(self, pe, z):
        pe.wait_ge(z["ready"], 1)
        n = R * 2
        for l in range(2):
            for s in range(2):
                ins = pe.transpose(z["tp"][:, l * 2 + s, :], z["raw"][l][s][:, :], self.g.ident[0:n, 0:n])
        ins.then_inc(z["turned"], 1)


def store(nc, g, out):
    with Phase(nc, "store") as ph:
        stored = ph.sem("stored")
        block = ph.block()

        @block.sync
        def _(sp):
            sp.dma_start(out[0:(T - 1) * P, :].rearrange("(t p) f -> p t f", p=P), g.x[:, 0:T - 1, :]).then_inc(stored, 16)
            sp.dma_start(out[(T - 1) * P:N, :], g.x[0:LAST, T - 1, :]).then_inc(stored, 16)
            sp.wait_ge(stored, 32)


class Persistent:

    def __init__(self, ctx, nc):
        def sb(name, shape, dt=F32):
            return ctx.enter_context(nc.sbuf_tensor(name, shape, dt))

        self.ctx = ctx
        self.x = sb("x", [P, T, D])
        self.pcol = sb("pcol", [P, 1])
        self.before = sb("before", [ROWS, 1], I32)
        self.typr = sb("typr", [ROWS, COLS])
        self.look = sb("look", [P, T, 8])
        self.first = sb("first", [P, T], I32)
        self.mean, self.rstd = sb("mean", [P, T]), sb("rstd", [P, T])
        self.ident = sb("ident", [P, P])
        self.nodes = sb("nodes", [P, NP])
        self.dstb = sb("dstb", [P, C])
        self.dsti, self.srci = sb("dsti", [P, C], I32), sb("srci", [P, C], I32)
        self.srct = sb("srct", [P, C], I32)
        self.same, self.apart = sb("same", [ROWS, COLS + 1]), sb("apart", [ROWS, COLS + 1])
        self.rowsame, self.rowapart = sb("rowsame", [8, 2, ROWS]), sb("rowapart", [8, 2, ROWS])
        self.walk = sb("walk", [1, LAG + STEPS, 2], I32)


def gnn_ffn(nc, x, src, dst, edge_type_8, w, out, stop=99):
    table0 = nc.dram_tensor("table0", [NP, R * D], F32).ap()
    tabs0 = nc.dram_tensor("tabs0", [NP, R * 4], F32).ap()
    tabd0 = nc.dram_tensor("tabd0", [NP, R * 4], F32).ap()
    table1 = nc.dram_tensor("table1", [NP, 512], F32).ap()
    tabd1 = nc.dram_tensor("tabd1", [NP, 16], F32).ap()
    table2 = nc.dram_tensor("table2", [NP, D], F32).ap()
    tabd2 = nc.dram_tensor("tabd2", [NP, 2], F32).ap()
    spread0, spread1, spread2 = (nc.dram_tensor(f"spread{l}", [ROWS * COLS + NP, width], F32).ap()
                                 for l, width in enumerate((R * 4, 16, 2)))
    src_low = nc.dram_tensor("src_low", [ROWS * COLS], BF16).ap()
    with ExitStack() as ctx:
        g = Persistent(ctx, nc)

        def tile_of(t):
            return g.x[:, ds(t, 1), :].rearrange("p a f -> p (a f)")

        setup(nc, g, x, src, dst, edge_type_8, src_low)
        node_starts(nc, g, [spread0, spread1, spread2])

        def normed_pair(dve, ex, link, i, rows, scaled=None):
            for u in range(2):
                normed(nc, g, link, rows[u][:, :], i * 2 + u)
                if scaled:
                    link(nc.vector.tensor_tensor(rows[u][:, :], rows[u][:, :], scaled[0][:, :], ALU.mult))
                    link(nc.vector.tensor_tensor(rows[u][:, :], rows[u][:, :], scaled[1][:, :], ALU.add))
                dve.sem_inc(ex.rows_ready, 1)

        node_stats(nc, g, "p0", False)
        conv, hd = w["L0_gnn_conv_weights"], D // 4
        with ExitStack() as c0:
            alpha0 = c0.enter_context(nc.sbuf_tensor("alpha0", [P, C, 4], F32))
            with ExitStack() as c00:
                w0 = c00.enter_context(nc.sbuf_tensor("w0", [P, 2, R * D], F32))
                rt0 = c00.enter_context(nc.sbuf_tensor("rt0", [P, 2, NP], F32))
                project(nc, g, "p0", 2, R * D, R * 4, w0,
                        lambda t: [(t[:, k, :].rearrange("p (r d) -> p r d", d=hd),
                                    conv.rearrange("r h (k i) d -> k i (r h) d", i=P)[k]) for k in range(2)],
                        lambda t: [(t[:, s, :], row_of(w[n].rearrange("r h d -> (r h d)"))) for s, n in enumerate(("L0_gnn_attn_l", "L0_gnn_attn_r"))],
                        normed_pair, False, None, tabs0, tabd0, rt0, False, lambda ph: PlainTile(ph, 1))
                edge_alphas(nc, g, "e0", 4, R * 4, False, True, tabs0.rearrange("n (r h) -> (n r) h", h=4), tabd0, spread0, None,
                            lambda ph: Features(nc, g, ph, rt0, w0, table0), alpha0)
            acc0 = c0.enter_context(nc.sbuf_tensor("acc0", [P, T, D], F32))
            edge_messages(nc, g, "e0", 4, D, False, g.srct, table0.rearrange("n (r f) -> (n r) f", f=D), alpha0, acc0)
            xt0 = c0.enter_context(nc.sbuf_tensor("xt0", [P, 2, NP], F32))
            wts0 = c0.enter_context(nc.sbuf_tensor("wts0", [P, R, T], F32))

            def prep_f0(dve, ex, link, i, u, rows):
                normed(nc, g, link, rows[:, :], i * 2 + u)
                link(nc.vector.tensor_tensor(rows[:, :], rows[:, :], ex.tiles[0][:, :], ALU.mult))
                link(nc.vector.tensor_tensor(rows[:, :], rows[:, :], ex.tiles[1][:, :], ALU.add))

            def update0(dve, link, consts):
                link(nc.vector.tensor_tensor(g.x[:, :, :], g.x[:, :, :], acc0[:, :, :], ALU.add))
                link(nc.vector.tensor_tensor(g.x[:, :, :], g.x[:, :, :], consts[0].rearrange("p (a f) -> p a f", a=1).to_broadcast([P, T, D]), ALU.add))

            node_stats(nc, g, "f0", True, alloc=lambda ph: [(ph.sb("bias", [P, D])[:, :], row_of(w["L0_gnn_h_bias"]))], update=update0)
            if stop == 0:
                store(nc, g, out)
                return
            route(nc, g, "f0", prep_f0, 3,
                  lambda ph: PlainTile(ph, 0, (w["L0_ffn_gamma"], w["L0_ffn_beta"], w["L0_ffn_br"])),
                  w["L0_ffn_Wr"], w["L0_ffn_b2"], True, xt0, wts0)
            if stop > 1:
                experts(nc, g, "f0", [(2, 4)], [w["L0_ffn_W1"], w["L0_ffn_W2"]], False, GeluParams(nc, g, w["L0_ffn_b1"]), xt0, wts0)
        if stop <= 2:
            store(nc, g, out)
            return

        node_stats(nc, g, "p1", True)
        with ExitStack() as c1:
            alpha1 = c1.enter_context(nc.sbuf_tensor("alpha1", [P, C, 8], F32))
            with ExitStack() as c11:
                w1 = c11.enter_context(nc.sbuf_tensor("w1", [P, 2, 512], F32))
                project(nc, g, "p1", 2, 512, 8, w1,
                        lambda t: [(t[:, :, :], w["L1_gnn_W1"].rearrange("(k i) f -> i k f", i=P))],
                        lambda t: [(t[:, s, :], row_of(w[n].rearrange("h d -> (h d)"))) for s, n in enumerate(("L1_gnn_att_src1", "L1_gnn_att_dst1"))],
                        lambda dve, ex, link, i, rows: normed_pair(dve, ex, link, i, rows, ex.tiles),
                        True, table1, None, tabd1, None, True, lambda ph: PlainTile(ph, 3, (w["L1_gnn_ln_w"], w["L1_gnn_ln_b"])))
            edge_alphas(nc, g, "e1", 8, 16, True, False, None, tabd1, spread1, src_low, None, alpha1)
            acc1 = c1.enter_context(nc.sbuf_tensor("acc1", [P, T, 520], F32))
            edge_messages(nc, g, "e1", 8, 512, True, g.srci, table1, alpha1, acc1)

            def prep_p2(dve, ex, link, i, rows):
                for u in range(2):
                    t, row, neg = i * 2 + u, rows[u][:, :], ex.neg[u][:, :]
                    dve.wait_ge(ex.landed[u], (i + 1) * 16)
                    add_self_loop(nc, link, ex, row, ex.own[u][:, :], acc1[:, ds(t, 1), :].rearrange("p a f -> p (a f)"), 8, 512)
                    dve.sem_inc(ex.own_free, 1)
                    link(nc.vector.tensor_tensor(row, row, ex.tiles[0][:, :], ALU.add))
                    link(nc.vector.tensor_scalar(neg, row, 0.0, None, ALU.min))
                    dve.sem_inc(ex.neg_ready, 1)
                    link(nc.vector.tensor_scalar(row, row, 0.0, -1.0, ALU.max, ALU.add))
                for u in range(2):
                    dve.wait_ge(ex.exp_done, i * 2 + (u + 1))
                    link(nc.vector.tensor_tensor(rows[u][:, :], rows[u][:, :], ex.neg[u][:, :], ALU.add))
                    dve.sem_inc(ex.rows_ready, 1)

            w2 = c1.enter_context(nc.sbuf_tensor("w2", [P, 4, D], F32))
            project(nc, g, "p2", 4, D, 1, w2,
                    lambda t: [(t[:, :, :], w["L1_gnn_W2"].rearrange("(k i) f -> i k f", i=P))],
                    lambda t: [(t[:, s, :], row_of(w[n].rearrange("h d -> (h d)"))) for s, n in enumerate(("L1_gnn_att_src2", "L1_gnn_att_dst2"))],
                    prep_p2, True, table2, None, tabd2, None, True, lambda ph: LoadedTile(ph, g, 7, (w["L1_gnn_b1"],), table1))
        with ExitStack() as c2:
            alpha2 = c2.enter_context(nc.sbuf_tensor("alpha2", [P, C, 1], F32))
            edge_alphas(nc, g, "e2", 1, 2, True, False, None, tabd2, spread2, src_low, None, alpha2)
            acc2 = c2.enter_context(nc.sbuf_tensor("acc2", [P, T, D + 1], F32))
            edge_messages(nc, g, "e2", 1, D, True, g.srci, table2, alpha2, acc2)
            xt1 = c2.enter_context(nc.sbuf_tensor("xt1", [P, 2, NP], F32))
            wts1 = c2.enter_context(nc.sbuf_tensor("wts1", [P, R, T], F32))

            def update1(dve, link, tiles):
                own, bias = tiles
                aself = wts1[:, 0, :].rearrange("p (t a) -> p t a", a=1)
                link(nc.vector.tensor_scalar(aself, acc2[:, :, D:D + 1], -1.0, 1.0, ALU.mult, ALU.add))
                link(nc.vector.tensor_tensor(own, own, aself.to_broadcast([P, T, D]), ALU.mult))
                for more in (own, acc2[:, :, 0:D], bias.rearrange("p (a f) -> p a f", a=1).to_broadcast([P, T, D])):
                    link(nc.vector.tensor_tensor(g.x[:, :, :], g.x[:, :, :], more, ALU.add))

            node_stats(nc, g, "f1", False, update=update1,
                       alloc=lambda ph: [(ph.sb("own", [P, T, D])[:, :, :], table2.rearrange("(t p) f -> p t f", p=P)),
                                         (ph.sb("bias", [P, D])[:, :], row_of(w["L1_gnn_b2"]))])
            route(nc, g, "f1", lambda dve, ex, link, i, u, rows: normed(nc, g, link, rows[:, :], i * 2 + u), 1,
                  lambda ph: PlainTile(ph, 0, (w["L1_ffn_br"],)),
                  w["L1_ffn_Wr"], w["L1_ffn_bo"], False, xt1, wts1)
            p = {k: w[f"L1_ffn_{k}"] for k in ("b1", "g1", "be1", "m1", "v1", "b2", "g2", "be2", "m2", "v2")}
            experts(nc, g, "f1", [(2, 2), (2, 2)], [w["L1_ffn_W1"], w["L1_ffn_W2"], w["L1_ffn_Wo"]], True,
                    NormParams(nc, g, [[p[k + str(l)] for k in ("b", "g", "be", "m", "v")] for l in (1, 2)]), xt1, wts1)
        store(nc, g, out)


_INS = ["x", "src", "dst", "edge_type_8"]
_WEIGHTS = ["L0_gnn_conv_weights", "L0_gnn_attn_l", "L0_gnn_attn_r", "L0_gnn_h_bias", "L0_ffn_gamma", "L0_ffn_beta",
            "L0_ffn_Wr", "L0_ffn_br", "L0_ffn_W1", "L0_ffn_b1", "L0_ffn_W2", "L0_ffn_b2", "L1_gnn_ln_w", "L1_gnn_ln_b",
            "L1_gnn_W1", "L1_gnn_att_src1", "L1_gnn_att_dst1", "L1_gnn_b1", "L1_gnn_W2", "L1_gnn_att_src2",
            "L1_gnn_att_dst2", "L1_gnn_b2", "L1_ffn_Wr", "L1_ffn_br", "L1_ffn_W1", "L1_ffn_b1", "L1_ffn_g1", "L1_ffn_be1",
            "L1_ffn_m1", "L1_ffn_v1", "L1_ffn_W2", "L1_ffn_b2", "L1_ffn_g2", "L1_ffn_be2", "L1_ffn_m2", "L1_ffn_v2",
            "L1_ffn_Wo", "L1_ffn_bo"]


def kernel(**inputs):
    import numpy as _np
    import concourse.bacc as _bacc
    from concourse import mybir as _mybir
    from concourse.bass_utils import run_bass_kernel_spmd as _run

    nc = _bacc.Bacc("TRN2", target_bir_lowering=False, num_devices=1)
    arrays, args = {}, {}
    for name in _INS + _WEIGHTS:
        a = _np.ascontiguousarray(inputs[name])
        arrays[f"in_{name}_dram"] = a
        args[name] = nc.dram_tensor(f"in_{name}_dram", a.shape, _mybir.dt.from_np(a.dtype), kind="ExternalInput").ap()
    out = nc.dram_tensor("out_0_dram", (N, D), _mybir.dt.float32, kind="ExternalOutput").ap()
    gnn_ffn(nc, *[args[n] for n in _INS], {n: args[n] for n in _WEIGHTS}, out, STOP)
    r = _run(nc, [arrays], core_ids=[0])
    return r.results[0]["out_0_dram"]
```
